# Optimizing a Trainium2 kernel written in Bass

```python
import numpy as np
import jax
import jax.numpy as jnp

def _softmax(x, axis=-1):
    return jax.nn.softmax(x, axis=axis)

def _gelu(x):
    return jax.nn.gelu(x, approximate=True)

def _silu(x):
    return jax.nn.silu(x)

def _sigmoid(x):
    return jax.nn.sigmoid(x)

def _layernorm(x, axis=-1, eps=1e-05):
    m = jnp.mean(x, axis=axis, keepdims=True)
    v = jnp.var(x, axis=axis, keepdims=True)
    return (x - m) / jnp.sqrt(v + eps)

def _scatter_add(tgt, idx, src, axis=0):
    return tgt.at[idx].add(src)

def _segment_sum(src, seg, n):
    return jax.ops.segment_sum(src, seg, n)
kernel_name = 'mk_prb_d1_jaxref_r8_ffd176'

def setup_inputs(seed: int=0):
    np.random.seed(seed)
    _w = jnp.asarray

    def _L0_attn_setup():
        import jax, jax.numpy as jnp
        import numpy as np
        HIDDEN = 128
        NUM_HEADS = 16
        HEAD = HIDDEN // NUM_HEADS
        LEFT = 64
        RIGHT = 8
        NUM_POS = LEFT + RIGHT + 1
        key = jax.random.key(seed)
        ks = jax.random.split(key, 10)
        s = 1.0 / np.sqrt(HIDDEN)
        return {'hidden_states': jax.random.normal(ks[0], (4, 256, HIDDEN), jnp.float32), 'Wq': jax.random.normal(ks[1], (HIDDEN, HIDDEN), jnp.float32) * s, 'bq': jax.random.normal(ks[2], (HIDDEN,), jnp.float32) * 0.01, 'Wk': jax.random.normal(ks[3], (HIDDEN, HIDDEN), jnp.float32) * s, 'bk': jax.random.normal(ks[4], (HIDDEN,), jnp.float32) * 0.01, 'Wv': jax.random.normal(ks[5], (HIDDEN, HIDDEN), jnp.float32) * s, 'bv': jax.random.normal(ks[6], (HIDDEN,), jnp.float32) * 0.01, 'Wo': jax.random.normal(ks[7], (HIDDEN, HIDDEN), jnp.float32) * s, 'bo': jax.random.normal(ks[8], (HIDDEN,), jnp.float32) * 0.01, 'dist_emb': jax.random.normal(ks[9], (NUM_POS, HEAD), jnp.float32)}
    _L0_attn_in = _L0_attn_setup()

    def _L0_ffn_setup():
        import jax, jax.numpy as jnp
        import numpy as np
        D_MODEL = 128
        M = 64
        INNER = 16
        key = jax.random.key(seed)
        ks = jax.random.split(key, 9)

        def init(k, shape, fan_in):
            bound = 1.0 / np.sqrt(fan_in)
            return jax.random.uniform(k, shape, jnp.float32, -bound, bound)
        x = jax.random.normal(ks[0], (16, 512, D_MODEL), dtype=jnp.float32)
        Win = init(ks[1], (D_MODEL, M), D_MODEL)
        bin_ = init(ks[2], (M,), D_MODEL)
        W1 = init(ks[3], (M, INNER), 1)
        b1 = init(ks[4], (M, INNER), 1)
        W2 = init(ks[5], (M, INNER), INNER)
        b2 = init(ks[6], (M,), INNER)
        Wout = init(ks[7], (M, D_MODEL), M)
        bout = init(ks[8], (D_MODEL,), M)
        return {'x': x, 'Win': Win, 'bin_': bin_, 'W1': W1, 'b1': b1, 'W2': W2, 'b2': b2, 'Wout': Wout, 'bout': bout}
    _L0_ffn_in = _L0_ffn_setup()
    _d = {'L0_attn_hidden_states': _L0_attn_in['hidden_states'], 'L0_attn_Wq': _L0_attn_in['Wq'], 'L0_attn_bq': _L0_attn_in['bq'], 'L0_attn_Wk': _L0_attn_in['Wk'], 'L0_attn_bk': _L0_attn_in['bk'], 'L0_attn_Wv': _L0_attn_in['Wv'], 'L0_attn_bv': _L0_attn_in['bv'], 'L0_attn_Wo': _L0_attn_in['Wo'], 'L0_attn_bo': _L0_attn_in['bo'], 'L0_attn_dist_emb': _L0_attn_in['dist_emb'], 'L0_ffn_Win': _L0_ffn_in['Win'], 'L0_ffn_bin_': _L0_ffn_in['bin_'], 'L0_ffn_W1': _L0_ffn_in['W1'], 'L0_ffn_b1': _L0_ffn_in['b1'], 'L0_ffn_W2': _L0_ffn_in['W2'], 'L0_ffn_b2': _L0_ffn_in['b2'], 'L0_ffn_Wout': _L0_ffn_in['Wout'], 'L0_ffn_bout': _L0_ffn_in['bout']}
    _x0 = _d['L0_attn_hidden_states']
    _d['L0_attn_hidden_states'] = jax.random.normal(jax.random.fold_in(jax.random.key(seed), 1), (8, 512, 128), dtype=_x0.dtype)
    del _x0
    return _d

def reference(L0_attn_hidden_states, L0_attn_Wq, L0_attn_bq, L0_attn_Wk, L0_attn_bk, L0_attn_Wv, L0_attn_bv, L0_attn_Wo, L0_attn_bo, L0_attn_dist_emb, L0_ffn_Win, L0_ffn_bin_, L0_ffn_W1, L0_ffn_b1, L0_ffn_W2, L0_ffn_b2, L0_ffn_Wout, L0_ffn_bout):

    def _L0_attn_ref(hidden_states, Wq, bq, Wk, bk, Wv, bv, Wo, bo, dist_emb):
        import jax, jax.numpy as jnp
        import numpy as np
        HIDDEN = 128
        NUM_HEADS = 16
        HEAD = HIDDEN // NUM_HEADS
        LEFT = 64
        RIGHT = 8
        NUM_POS = LEFT + RIGHT + 1
        B, L, H = hidden_states.shape
        scale = 1.0 / np.sqrt(HEAD)

        def proj(W, b):
            return (hidden_states @ W.T + b).reshape(B, L, NUM_HEADS, HEAD).transpose(0, 2, 1, 3)
        q = proj(Wq, bq)
        k = proj(Wk, bk)
        v = proj(Wv, bv)
        attn = jnp.einsum('bhld,bhrd->bhlr', q, k) * scale
        dist = jnp.arange(L)[None, :] - jnp.arange(L)[:, None]
        dist = jnp.clip(dist, -LEFT, RIGHT) + LEFT
        pos_emb = dist_emb[dist]
        rel = jnp.einsum('bhld,lrd->bhlr', q, pos_emb) * scale
        attn = jax.nn.softmax(attn + rel, axis=-1)
        out = jnp.einsum('bhlr,bhrd->bhld', attn, v)
        out = out.transpose(0, 2, 1, 3).reshape(B, L, H)
        return out @ Wo.T + bo

    def _L0_ffn_ref(x, Win, bin_, W1, b1, W2, b2, Wout, bout):
        import jax, jax.numpy as jnp
        import numpy as np
        D_MODEL = 128
        M = 64
        INNER = 16
        s = jnp.einsum('btd,dm->btm', x, Win) + bin_
        h = jax.nn.relu(s[..., None] * W1 + b1)
        g = jnp.einsum('btmh,mh->btm', h, W2) + b2
        out = jnp.einsum('btm,md->btd', g, Wout) + bout
        return out
    x = L0_attn_hidden_states
    xn = _layernorm(x, axis=-1)
    x = x + _L0_attn_ref(xn, L0_attn_Wq, L0_attn_bq, L0_attn_Wk, L0_attn_bk, L0_attn_Wv, L0_attn_bv, L0_attn_Wo, L0_attn_bo, L0_attn_dist_emb) + _L0_ffn_ref(xn, L0_ffn_Win, L0_ffn_bin_, L0_ffn_W1, L0_ffn_b1, L0_ffn_W2, L0_ffn_b2, L0_ffn_Wout, L0_ffn_bout)
    return x

_drawn_inputs = setup_inputs


def setup_inputs(seed=0):
    import zlib

    import numpy as np

    out = dict(_drawn_inputs(seed))
    spreads = {}
    factors = {'L0_attn_bq': 37.514,
     'L0_attn_bk': 64.0,
     'L0_attn_bv': 5.359,
     'L0_attn_bo': 5.553,
     'L0_ffn_bin_': 8.0}
    for name, (base, spread) in spreads.items():
        noise = np.random.default_rng([zlib.crc32(name.encode()), seed]).standard_normal(out[name].shape)
        drawn = base * np.exp(spread * noise) if base else spread * noise
        out[name] = jnp.asarray(drawn.astype(out[name].dtype))
    for name, factor in factors.items():
        out[name] = (out[name] * factor).astype(out[name].dtype)
    return out
```

```python
from contextlib import ExitStack

import concourse.bass as bass
from concourse import mybir

F32 = mybir.dt.float32
BF16 = mybir.dt.bfloat16
F16 = mybir.dt.float16
ALU = mybir.AluOpType
ACT = mybir.ActivationFunctionType
AX_X = mybir.AxisListType.X

B, L, H = 8, 512, 128
NH, D = 16, 8
LEFT, RIGHT = 64, 8
NPOS = LEFT + RIGHT + 1
M, INNER = 64, 16
P = 128
LT = L // P
BLK = P // D
NBLK = L // BLK
G = 8
NG = NH // G
Q4 = 4
NQ = G // Q4
LN_EPS = 1e-5
SCALE = float(D) ** -0.5
PROD = [(0, 0), (0, 1), (0, 2), (1, 0), (1, 1), (2, 0)]
KROWS = len(PROD) * D
MROW = KROWS
K_MID, K_LEFT, K_RIGHT = range(3)
KW = L + 2 * (L - P)
YOFF = P + LEFT - BLK
YLEN = YOFF + P + BLK
XOFF = YOFF + BLK - 1
XLEN = YLEN + BLK - 1
TPROD = [(0, 0), (0, 1), (1, 0)]


def tile_kind(rt, lt):
    return K_MID if rt == lt else K_RIGHT if lt < rt else K_LEFT


def mixed_blocks(rt, lt):
    out = []
    for g in range(P // BLK):
        d0 = (lt - rt) * P + g * BLK
        right = -d0 - (BLK - 1) >= RIGHT
        left = P - 1 - d0 <= -LEFT
        if not (right or left):
            out.append(g)
    return out


def build(nc, hidden, Wq, bq, Wk, bk, Wv, bv, Wo, bo, emb, Win, bin_, W1, b1, W2, b2, Wout, bout, out):
    qk_d = nc.dram_tensor("qk_parts", [4, 3, P, B, L], BF16, kind="Internal").ap()
    qd_d = nc.dram_tensor("q_blocked", [P, B, BLK, NBLK], BF16, kind="Internal").ap()
    qh_d = nc.dram_tensor("q_half_parts", [NG, 2, G * D, B, BLK, NBLK], F16, kind="Internal").ap()
    v_d = nc.dram_tensor("v_rows", [P, B, LT, NH, 32], F32, kind="Internal").ap()
    m_d = nc.dram_tensor("max_rows", [2, G, NBLK, BLK], BF16, kind="Internal").ap()
    ones_d = nc.dram_tensor("ones_row", [P, 2 * G * KW // P], BF16, kind="Internal").ap()
    x_t = hidden.rearrange("b (t p) f -> p b t f", p=P)
    o_t = out.rearrange("b (t p) f -> p b t f", p=P)

    with ExitStack() as whole:
        def sb(ctx, name, shape, dt):
            return ctx.enter_context(nc.sbuf_tensor(name, shape, dt))

        base = sb(whole, "base", [P, B, LT, H], F32)
        s_all = sb(whole, "s_all", [P, B, L // 2], F32)
        ident = sb(whole, "ident", [P, P], F32)
        toep = sb(whole, "toep", [P, 3, 2, YLEN], F16)
        wo_pad = sb(whole, "wo_pad", [P, NH // Q4, H], F32)
        wout2 = sb(whole, "wout2", [P, 2, H], F32)
        den_sel = sb(whole, "den_sel", [P, P], F32)
        w1c = sb(whole, "w1c", [P, INNER], F32)
        b1c = sb(whole, "b1c", [P, INNER], F32)
        w2c = sb(whole, "w2c", [P, INNER], F32)
        b2c = sb(whole, "b2c", [P, 1], F32)

        prepare(nc, sb, locals())
        attend(nc, sb, locals())


def prepare(nc, sb, t):
    x_t, base, s_all, ident, toep = t["x_t"], t["base"], t["s_all"], t["ident"], t["toep"]
    wo_pad, wout2, den_sel = t["wo_pad"], t["wout2"], t["den_sel"]
    with ExitStack() as ctx:
        def pb(name, shape, dt=F32):
            return ctx.enter_context(nc.psum_tensor(name, shape, dt))

        def sem(name):
            return ctx.enter_context(nc.semaphore(name))

        wraw = sb(ctx, "wraw", [P, 4, H], F32)
        wT = sb(ctx, "wT", [P, 4, H], F32)
        win = sb(ctx, "win", [P, M], F32)
        colb = sb(ctx, "colb", [P, 8], F32)
        colc = sb(ctx, "colc", [P, 4], F32)
        rows = sb(ctx, "rows", [P, 4, H], F32)
        emb_sb = sb(ctx, "emb_sb", [P, D], F32)
        ep = sb(ctx, "ep", [D, 3, XLEN], F32)
        eph = sb(ctx, "eph", [D, 3, 2, XLEN], F16)
        xn = sb(ctx, "xn", [P, 2, LT, H], F32)
        xT = sb(ctx, "xT", [P, 2, L], F32)
        stats = sb(ctx, "stats", [P, B, LT, 6], F32)
        mv = sb(ctx, "mv", [P, B, LT, 2], F32)
        var = sb(ctx, "var", [P, B, LT], F32)
        std = sb(ctx, "std", [P, B, LT], F32)
        rs0 = sb(ctx, "rs0", [P, B, LT], F32)
        tmp = sb(ctx, "tmp", [P, 2, B, LT], F32)
        rstd = sb(ctx, "rstd", [P, B, LT], F32)
        qkf = sb(ctx, "qkf", [P, 2, 4, L], F32)
        rem = sb(ctx, "rem", [P, 2, 4, L], F32)
        parts = sb(ctx, "parts", [P, 2, 4, 3, L], BF16)
        qd = sb(ctx, "qd", [P, 2, BLK, NBLK], BF16)
        qh = sb(ctx, "qh", [P, 2, 2, BLK, NBLK], F16)
        vrow = sb(ctx, "vrow", [P, 2, LT, NH, 32], F32)

        ps_t = pb("ps_t", [P, 2, L])
        ps_q = pb("ps_q", [P, L])
        ps_k = pb("ps_k", [P, L])
        ps_v = pb("ps_v", [P, 2, L])
        ps_s = pb("ps_s", [P, L])
        ps_w = pb("ps_w", [P, L])

        s_cst, s_x, s_ident, s_selz, s_wT, s_wTc = (sem(n) for n in ("c_cst", "c_x", "c_ident", "c_selz", "c_wT", "c_wTc"))
        s_ebT, s_ep, s_tab, s_pad, s_col, s_vec = (sem(n) for n in ("c_ebT", "c_ep", "c_tab", "c_pad", "c_col", "c_vec"))
        s_ln, s_t, s_tc, s_qk, s_v, s_s = (sem(n) for n in ("c_ln", "c_t", "c_tc", "c_qk", "c_v", "c_s"))
        s_qkf, s_sc, s_vc, s_hi, s_r, s_mid, s_lo, s_act = (sem(n) for n in ("c_qkf", "c_sc", "c_vc", "c_hi", "c_r", "c_mid", "c_lo", "c_act"))
        s_var = sem("c_var")
        s_out = [sem("c_out0"), sem("c_out1")]
        NCST = 15
        NST = 16 * 5

        with nc.Block() as block:
            @block.sync
            def _(sp):
                for n, w in enumerate(("Wq", "Wk", "Wv", "Wo")):
                    sp.dma_start(wraw[:, n], t[w]).then_inc(s_cst, 16)
                sp.dma_start(win[:], t["Win"]).then_inc(s_cst, 16)
                for b in range(B):
                    sp.dma_start(base[:, b], x_t[:, b]).then_inc(s_x, 16)

                def on_rows(v, n):
                    return bass.AP(v.tensor, v.offset, [[0, n], [1, H]])

                for n, v in enumerate(("bv", "bo", "bout")):
                    sp.dma_start(rows[:, n], on_rows(t[v], P)).then_inc(s_cst, 16)
                sp.dma_start(colb[:, 0:1], t["bq"].rearrange("(p a) -> p a", a=1)).then_inc(s_cst, 16)
                sp.dma_start(colb[:, 1:2], t["bk"].rearrange("(p a) -> p a", a=1)).then_inc(s_cst, 16)
                for n, row in ((2, 0), (3, NPOS - 1)):
                    e = t["emb"][row]
                    sp.dma_start(colb[:, n:n + 1], bass.AP(e.tensor, e.offset, [[0, NH], [1, D], [1, 1]])).then_inc(s_cst, 16)
                sp.dma_start(emb_sb[0:NPOS, :], t["emb"]).then_inc(s_cst, 16)
                for h in range(2):
                    half = slice(M * h, M * h + M)
                    sp.dma_start(colb[half, 4:5], t["bin_"].rearrange("(p a) -> p a", a=1)).then_inc(s_cst, 16)
                    sp.dma_start(t["b2c"][half], t["b2"].rearrange("(p a) -> p a", a=1)).then_inc(s_pad, 16)
                    sp.dma_start(t["w1c"][half], t["W1"]).then_inc(s_pad, 16)
                    sp.dma_start(t["b1c"][half], t["b1"]).then_inc(s_pad, 16)
                    sp.dma_start(t["w2c"][half], t["W2"]).then_inc(s_pad, 16)
                sp.wait_ge(s_ep, 3)
                for j in range(BLK):
                    sp.dma_start(toep[j * D:(j + 1) * D], eph[:, :, :, BLK - 1 - j:BLK - 1 - j + YLEN]).then_inc(s_pad, 16)
                sp.wait_ge(s_wTc, 1)
                sp.wait_ge(s_selz, 4)
                for h in range(2):
                    sp.dma_start(wout2[M * h:M * h + M, h], t["Wout"]).then_inc(s_pad, 16)
                for h in range(NH):
                    sp.dma_start(wo_pad[32 * (h % Q4):32 * (h % Q4) + D, h // Q4], wT[h * D:(h + 1) * D, 3]).then_inc(s_pad, 16)
                sp.wait_ge(s_pad, 16 * (10 + BLK + NH))

                def store(n, s):
                    sp.wait_ge(s_lo, 5 * n + 5)
                    sp.wait_ge(s_hi, 6 * n + 6)
                    sp.dma_start(t["qk_d"][:, :, :, n].rearrange("n a p l -> p (n a) l"),
                                 parts[:, s].rearrange("p n a l -> p (n a) l")).then_inc(s_out[s], 16)
                    sp.dma_start(t["qd_d"][:, n], qd[:, s]).then_inc(s_out[s], 16)
                    for hg in range(NG):
                        sp.dma_start(t["qh_d"][hg, :, :, n].rearrange("a p j g -> p a (j g)"),
                                     qh[hg * G * D:(hg + 1) * G * D, s].rearrange("p a j g -> p a (j g)")).then_inc(s_out[s], 16)
                    sp.wait_ge(s_vc, n + 3)
                    sp.dma_start(t["v_d"][:, n], vrow[:, s]).then_inc(s_out[s], 16)

                with sp.Fori(0, B // 2) as i:
                    for s in range(2):
                        store(2 * i + s, s)
                for s in range(2):
                    sp.wait_ge(s_out[s], NST * (B // 2) + 1)

            @block.gpsimd
            def _(pool):
                nc.gpsimd.memset(ident[:], 0.0).then_inc(s_selz, 1)
                nc.gpsimd.memset(den_sel[:], 0.0).then_inc(s_selz, 1)
                nc.gpsimd.memset(wo_pad[:], 0.0).then_inc(s_selz, 1)
                nc.gpsimd.memset(wout2[:], 0.0).then_inc(s_selz, 1)
                pool.wait_ge(s_selz, 4)
                nc.gpsimd.affine_select(out=ident[:], in_=ident[:], compare_op=ALU.not_equal, fill=1.0, base=0,
                                        pattern=[[-1, P]], channel_multiplier=1).then_inc(s_ident, 1)
                sel = den_sel[:].rearrange("p (h i) -> p h i", h=Q4)
                nc.gpsimd.affine_select(out=sel, in_=sel, compare_op=ALU.not_equal, fill=1.0, base=-D,
                                        pattern=[[-32, Q4], [0, 32]], channel_multiplier=1).then_inc(s_ident, 1)

            @block.tensor
            def _(pe):
                pe.wait_ge(s_cst, 16 * NCST)
                pe.wait_ge(s_ident, 2)
                for n in range(4):
                    w = nc.tensor.transpose(ps_w[:, n * H:(n + 1) * H], wraw[:, n], ident[:])
                w.then_inc(s_wT, 1)
                nc.tensor.transpose(ps_s[0:D, 0:NPOS], emb_sb[0:NPOS, :], ident[0:NPOS, 0:NPOS]).then_inc(s_ebT, 1)
                pe.wait_ge(s_wTc, 1)
                pe.wait_ge(s_ep, 1)
                with pe.Fori(0, B // 2) as i:
                    for s in range(2):
                        b = 2 * i + s
                        pe.wait_ge(s_ln, b + 1)
                        pe.wait_ge(s_tc, b + 1)
                        for n in range(LT):
                            m = nc.tensor.transpose(ps_t[:, s, n * P:(n + 1) * P], xn[:, s, n], ident[:])
                        m.then_inc(s_t, 1)
                        pe.wait_ge(s_tc, b + 2)
                        pe.wait_ge(s_qkf, 4 * b + 1)
                        nc.tensor.matmul(ps_q[:], wT[:, 0], xT[:, s], start=True, stop=True).then_inc(s_qk, 1)
                        nc.tensor.matmul(ps_k[:], wT[:, 1], xT[:, s], start=True, stop=True).then_inc(s_qk, 1)
                        pe.wait_ge(s_vc, b + 1)
                        for n in range(LT):
                            m = nc.tensor.matmul(ps_v[:, s, n * P:(n + 1) * P], xT[:, s, n * P:(n + 1) * P], wT[:, 2],
                                                 start=(n == 0), stop=True, skip_group_check=True)
                        m.then_inc(s_v, 1)
                        pe.wait_ge(s_sc, b + 1)
                        for h in range(2):
                            m = nc.tensor.matmul(ps_s[M * h:M * h + M, 0:L // 2], win[:], xT[:, s, h * (L // 2):(h + 1) * (L // 2)],
                                                 start=True, stop=True)
                        m.then_inc(s_s, 1)

            @block.vector
            def _(dve):
                cnt = [0]

                def link(ins):
                    cnt[0] += 1
                    ins.then_inc(s_vec, 1)
                    dve.wait_ge(s_vec, cnt[0])

                dve.sem_inc(s_tc, 1)
                dve.sem_inc(s_sc, 1)
                dve.sem_inc(s_vc, 2)
                nc.vector.memset(vrow[:], 0.0).then_inc(s_vec, 1)
                cnt[0] += 1
                dve.wait_ge(s_cst, 16 * NCST)
                nc.vector.tensor_scalar(colc[:, 0:1], colb[:, 0:1], SCALE, None, ALU.mult).then_inc(s_col, 1)
                nc.vector.tensor_copy(colc[:, 1:2], colb[:, 1:2]).then_inc(s_col, 1)
                nc.vector.tensor_tensor(colc[:, 2:3], colb[:, 1:2], colb[:, 2:3], ALU.add).then_inc(s_col, 1)
                nc.vector.tensor_tensor(colc[:, 3:4], colb[:, 1:2], colb[:, 3:4], ALU.add).then_inc(s_col, 1)
                link(nc.vector.tensor_tensor(rows[:, 3], rows[:, 1], rows[:, 2], ALU.add))
                dve.wait_ge(s_vec, 1)
                link(nc.vector.memset(vrow[:, :, :, :, D:D + 1], 1.0))
                dve.wait_ge(s_wT, 1)
                nc.vector.tensor_copy(wT[:].rearrange("p n f -> p (n f)"), ps_w[:]).then_inc(s_wTc, 1)
                dve.wait_ge(s_ebT, 1)
                band0 = XOFF - LEFT
                link(nc.vector.memset(ep[:, 0], 0.0))
                nc.vector.tensor_copy(ep[:, 0, band0:band0 + NPOS], ps_s[0:D, 0:NPOS]).then_inc(s_ep, 1)
                dve.wait_ge(s_ep, 1)
                e_l, e_r = ep[:, 0, band0:band0 + 1], ep[:, 0, band0 + NPOS - 1:band0 + NPOS]
                link(nc.vector.tensor_scalar(ep[:, 0, 0:band0], ep[:, 0, 0:band0], e_l, None, ALU.add))
                link(nc.vector.tensor_scalar(ep[:, 0, band0 + NPOS:XLEN], ep[:, 0, band0 + NPOS:XLEN], e_r, None, ALU.add))
                link(nc.vector.tensor_scalar(ep[:, K_LEFT], ep[:, 0], e_l, None, ALU.subtract))
                link(nc.vector.tensor_scalar(ep[:, K_RIGHT], ep[:, 0], e_r, None, ALU.subtract))
                nc.vector.tensor_copy(eph[:, :, 0], ep[:]).then_inc(s_ep, 1)
                dve.wait_ge(s_ep, 2)
                nc.vector.tensor_tensor(eph[:, :, 1], ep[:], eph[:, :, 0], ALU.subtract).then_inc(s_ep, 1)
                dve.wait_ge(s_x, 16 * B)
                for b in range(B):
                    for n in range(LT):
                        m = nc.vector.bn_stats(stats[:, b, n], base[:, b, n])
                link(m)
                for b in range(B):
                    for n in range(LT):
                        m = nc.vector.bn_aggr(mv[:, b, n], stats[:, b, n])
                link(m)
                nc.vector.tensor_scalar(var[:], mv[:, :, :, 1], LN_EPS, None, ALU.add).then_inc(s_var, 1)
                dve.wait_ge(s_var, 2)
                link(nc.vector.reciprocal(rs0[:], std[:]))
                link(nc.vector.tensor_tensor(tmp[:, 0], rs0[:], rs0[:], ALU.mult))
                link(nc.vector.tensor_tensor(tmp[:, 1], tmp[:, 0], var[:], ALU.mult))
                link(nc.vector.tensor_scalar(tmp[:, 0], tmp[:, 1], -0.5, 1.5, ALU.mult, ALU.add))
                link(nc.vector.tensor_tensor(rstd[:], rs0[:], tmp[:, 0], ALU.mult))
                with dve.Fori(0, B // 2) as i:
                    for s in range(2):
                        b = 2 * i + s
                        for n in range(LT):
                            m = nc.vector.tensor_scalar(xn[:, s, n], base[:, b, n], mv[:, b, n, 0:1], rstd[:, b, n:n + 1],
                                                        ALU.subtract, ALU.mult)
                        m.then_inc(s_ln, 1)
                        dve.wait_ge(s_t, b + 1)
                        nc.vector.tensor_copy(xT[:, s], ps_t[:, s]).then_inc(s_tc, 1)
                        nc.vector.tensor_tensor(base[:, b], base[:, b], rows[:, 3:4].broadcast_to([P, LT, H]), ALU.add)
                        for n in range(4):
                            dve.wait_ge(s_hi, 6 * b + n + 1)
                            nc.vector.tensor_tensor(rem[:, s, n], qkf[:, s, n], parts[:, s, n, 0], ALU.subtract).then_inc(s_r, 1)
                        dve.wait_ge(s_hi, 6 * b + 6)
                        nc.vector.tensor_tensor(qh[:, s, 1].rearrange("p j g -> p g j"), qkf[:, s, 0].rearrange("p (g j) -> p g j", j=BLK),
                                                qh[:, s, 0].rearrange("p j g -> p g j"), ALU.subtract).then_inc(s_lo, 1)
                        for n in range(4):
                            dve.wait_ge(s_mid, 4 * b + n + 1)
                            nc.vector.tensor_tensor(parts[:, s, n, 2], rem[:, s, n], parts[:, s, n, 1], ALU.subtract).then_inc(s_lo, 1)
                        dve.wait_ge(s_s, b + 1)
                        nc.vector.tensor_scalar(s_all[:, b], ps_s[:, 0:L // 2], colb[:, 4:5], None, ALU.add).then_inc(s_sc, 1)
                        dve.wait_ge(s_v, b + 1)
                        dve.wait_ge(s_out[s], NST * i + 1)
                        nc.vector.tensor_tensor(vrow[:, s, :, :, 0:D], ps_v[:, s].rearrange("p (n h d) -> p n h d", n=LT, h=NH),
                                                rows[:, 0:1].broadcast_to([P, LT, H]).rearrange("p n (h d) -> p n h d", h=NH),
                                                ALU.add).then_inc(s_vc, 1)

            @block.scalar
            def _(act):
                act.sem_inc(s_qkf, 1)
                for s in range(2):
                    act.sem_inc(s_out[s], 1)
                act.wait_ge(s_var, 1)
                nc.scalar.activation(std[:], var[:], ACT.Sqrt).then_inc(s_var, 1)
                act.wait_ge(s_col, 4)
                with act.Fori(0, B // 2) as i:
                    for s in range(2):
                        b = 2 * i + s
                        act.wait_ge(s_qk, 2 * b + 1)
                        act.wait_ge(s_vc, b + 1)
                        act.wait_ge(s_out[s], NST * i + 1)
                        nc.scalar.activation(qkf[:, s, 0], ps_q[:], ACT.Identity, bias=colc[:, 0:1], scale=SCALE).then_inc(s_qkf, 1)
                        act.wait_ge(s_qk, 2 * b + 2)
                        for n in range(1, 4):
                            nc.scalar.activation(qkf[:, s, n], ps_k[:], ACT.Identity, bias=colc[:, n:n + 1], scale=1.0).then_inc(s_qkf, 1)
                        for n in range(4):
                            act.wait_ge(s_qkf, 4 * b + n + 2)
                            nc.scalar.copy(parts[:, s, n, 0], qkf[:, s, n]).then_inc(s_hi, 1)
                        blocked = qkf[:, s, 0].rearrange("p (g j) -> p j g", j=BLK)
                        nc.scalar.copy(qd[:, s], blocked).then_inc(s_hi, 1)
                        nc.scalar.copy(qh[:, s, 0], blocked).then_inc(s_hi, 1)
                        for n in range(4):
                            act.wait_ge(s_r, 4 * b + n + 1)
                            nc.scalar.copy(parts[:, s, n, 1], rem[:, s, n]).then_inc(s_mid, 1)


def attend(nc, sb, t):
    base, s_all, ident, toep = t["base"], t["s_all"], t["ident"], t["toep"]
    wo_pad, wout2, den_sel = t["wo_pad"], t["wout2"], t["den_sel"]
    with ExitStack() as ctx:
        def pb(name, shape, dt=F32):
            return ctx.enter_context(nc.psum_tensor(name, shape, dt))

        def sem(name):
            return ctx.enter_context(nc.semaphore(name))

        qst = sb(ctx, "qst", [KROWS + 1, 2, G, L], BF16)
        kst = sb(ctx, "kst", [KROWS + 1, 2, G, KW], BF16)
        vt = sb(ctx, "vt", [P, 2, LT, G, 32], F32)
        bq = sb(ctx, "bq", [P, 2, 2, G * L], F16)
        bqa = sb(ctx, "bqa", [P, 2, G * L], F16)
        bd = sb(ctx, "bd", [G * D, 2, G * L], BF16)
        ka = sb(ctx, "ka", [G * D, 2, 3, L], BF16)
        prob = sb(ctx, "prob", [P, 2, LT * (P // BLK) * Q4 * BLK], F32)
        osb = sb(ctx, "osb", [P, NH // Q4, L], F32)
        rden = sb(ctx, "rden", [P, L], F32)
        s_cur = sb(ctx, "s_cur", [P, L // 2], F32)
        relu = sb(ctx, "relu", [P, 2, L // 2], F32)
        acc = sb(ctx, "acc", [P, 2, L // 2], F32)
        mcol = sb(ctx, "mcol", [P, 2, NBLK], F32)
        mrow = sb(ctx, "mrow", [NBLK, 2, P], BF16)
        ones = sb(ctx, "ones", [P, 2 * G * KW // P], BF16)

        ps_a = pb("ps_a", [P, 2, L])
        ps_b = pb("ps_b", [P, 2, 2 * L])
        ps_o = pb("ps_o", [P, L])
        ps_m = pb("ps_m", [P, L])

        d_a, d_b, d_m = ([sem(f"{n}{s}") for s in range(2)] for n in ("d_a", "d_b", "d_m"))
        s_cp = sem("s_cp")
        d_md = sem("d_md")
        s_zero, s_ones = sem("s_zero"), sem("s_ones")
        a_full, a_free = sem("a_full"), sem("a_free")
        b_full, e_done = sem("b_full"), sem("e_done")
        p_free = sem("p_free")
        o_free = sem("o_free")
        m_full, m_free = sem("m_full"), sem("m_free")
        o_done, mr_done = sem("o_done"), sem("mr_done")
        r_full, r_free = sem("r_full"), sem("r_free")
        s_vec, s_res, s_done = sem("s_vec"), sem("s_res"), sem("s_done")

        NDA = BLK + G + 3
        NDB = len(PROD) * 4 + 1 + BLK
        NU = NQ * LT * 2
        NP = NQ * LT
        APU = 3
        A_LAST = (NBLK - 1) // APU
        NMISC = 7

        def cols(kind, rt):
            return {K_MID: 0, K_LEFT: L, K_RIGHT: L + (L - P) - P}[kind] + rt * P

        def misc(b, i, last):
            return NMISC * b + 1 + (i - 1 if last and i > 4 else i)

        with nc.Block() as block:
            @block.sync
            def _(sp):
                def load_a(b, hg, s):
                    hd = slice(hg * G * D, (hg + 1) * G * D)
                    for j in range(BLK):
                        sp.dma_start(bqa[j * D:(j + 1) * D, s].rearrange("d (h j g) -> d h j g", h=G, j=BLK)[:, :, j],
                                     t["qh_d"][hg, 0, :, b, j].rearrange("(h d) g -> d h g", h=G)).then_inc(d_a[s], 16)
                    for h in range(G):
                        sp.dma_start(bd[h * D:(h + 1) * D, s, h * L:(h + 1) * L],
                                     t["qd_d"][hg * G * D + h * D:hg * G * D + (h + 1) * D, b].rearrange("p j g -> p (j g)")).then_inc(d_a[s], 16)
                    for n in range(3):
                        sp.dma_start(ka[:, s, n], t["qk_d"][1 + n, 0, hd, b]).then_inc(d_a[s], 16)

                def load_b(b, hg, s):
                    hd = slice(hg * G * D, (hg + 1) * G * D)
                    for n, (pq, pk) in enumerate(PROD):
                        r = slice(n * D, (n + 1) * D)
                        for dst, src in (
                            (qst[r, s], t["qk_d"][0, pq, hd, b]),
                            (kst[r, s, :, 0:L], t["qk_d"][1 + K_MID, pk, hd, b]),
                            (kst[r, s, :, L:2 * L - P], t["qk_d"][1 + K_LEFT, pk, hd, b, 0:L - P]),
                            (kst[r, s, :, 2 * L - P:KW], t["qk_d"][1 + K_RIGHT, pk, hd, b, P:L]),
                        ):
                            sp.dma_start(dst, src.rearrange("(h d) l -> d h l", h=G)).then_inc(d_b[s], 16)
                    sp.dma_start(vt[:, s], t["v_d"][:, b, :, hg * G:(hg + 1) * G]).then_inc(d_b[s], 16)
                    for j in range(BLK):
                        sp.dma_start(bq[j * D:(j + 1) * D, s].rearrange("d a (h j g) -> d (a h) j g", h=G, j=BLK)[:, :, j],
                                     t["qh_d"][hg, :, :, b, j].rearrange("a (h d) g -> d (a h) g", h=G)).then_inc(d_b[s], 16)

                def max_row(n, s):
                    sp.wait_ge(mr_done, n + 1)
                    sp.dma_start(t["m_d"][s].rearrange("h g j -> g h j"), mrow[:, s].rearrange("g (h j) -> g h j", h=G)).then_inc(d_md, 16)
                    sp.wait_ge(d_md, 16 * (n + 2))
                    sp.dma_start(qst[MROW:MROW + 1, s], t["m_d"][s].rearrange("h g j -> (h g j)").rearrange("(a h l) -> a h l", a=1, h=G)).then_inc(d_m[s], 16)

                def body(b, last):
                    for hg in range(NG):
                        o = 1 - hg
                        if not (last and hg == 1):
                            sp.wait_ge(p_free, 2 * NP * b + NP * hg + 2)
                            load_b(b + hg, o, o)
                        if not last:
                            sp.wait_ge(a_full, NBLK * (2 * b + hg + 1))
                            load_a(b + 1, hg, hg)
                        if not (last and hg == 1):
                            max_row(2 * b + hg + 1, o)

                sp.wait_ge(s_zero, 4)
                sp.wait_ge(s_ones, 1)
                sp.dma_start(t["ones_d"], ones[:]).then_inc(d_md, 16)
                sp.wait_ge(d_md, 16)
                sp.dma_start(kst[MROW:MROW + 1].rearrange("p s h k -> p (s h k)"),
                             t["ones_d"].rearrange("p k -> (p k)").rearrange("(a k) -> a k", a=1)).then_inc(s_ones, 16)
                load_a(0, 0, 0)
                load_b(0, 0, 0)
                load_a(0, 1, 1)
                max_row(0, 0)
                with sp.Fori(0, B - 1) as b:
                    body(b, False)
                body(B - 1, True)

            @block.gpsimd
            def _(pool):
                nc.gpsimd.memset(bqa[:].bitcast(F32), 0.0).then_inc(s_zero, 1)
                nc.gpsimd.memset(bd[:].bitcast(F32), 0.0).then_inc(s_zero, 1)
                with pool.Fori(0, B) as b:
                    pool.wait_ge(s_res, b + 1)
                    pool.dma_start(t["o_t"][:, b], base[:, b]).then_inc(s_done, 16)
                pool.wait_ge(s_done, 16 * B)

            @block.tensor
            def _(pe):
                def a_unit(a, g, s):
                    ps = ps_a[:, g % 2]
                    c0, c1 = max(0, g * BLK - LEFT), min(L, g * BLK + BLK + RIGHT)
                    pe.wait_ge(a_free, a + 1)
                    first = True
                    for kind, lo, hi in ((K_LEFT, 0, c0), (K_MID, c0, c1), (K_RIGHT, c1, L)):
                        if hi > lo:
                            nc.tensor.matmul(ps[:, lo:hi], bd[:, s, g::NBLK], ka[:, s, kind, lo:hi], start=first, stop=True,
                                             skip_group_check=True)
                            first = False
                    y = c0 - g * BLK + YOFF
                    nc.tensor.matmul(ps[:, c0:c1], bqa[:, s, g::NBLK], toep[:, K_MID, 0, y:y + c1 - c0], start=False, stop=True,
                                     skip_group_check=True).then_inc(a_full, 1)

                def b_unit(n, u, s):
                    hq, rt, half = u // (2 * LT), u // 2 % LT, u % 2
                    pe.wait_ge(e_done, n + 1)
                    for i in range(2):
                        lt = 2 * half + i
                        kind = tile_kind(rt, lt)
                        ps = ps_b[:, u % 2, i * L:(i + 1) * L]
                        by_head = ps.rearrange("p (g h j) -> p g h j", g=P // BLK, h=Q4)
                        for h in range(Q4):
                            m = nc.tensor.matmul(by_head[:, :, h], kst[:, s, hq * Q4 + h, cols(kind, rt):cols(kind, rt) + P],
                                                 qst[:, s, hq * Q4 + h, lt * P:(lt + 1) * P].rearrange("p (g j) -> p g j", j=BLK),
                                                 start=(h == 0), stop=True, skip_group_check=True)
                        for g in mixed_blocks(rt, lt):
                            blk = lt * (P // BLK) + g
                            y = rt * P - blk * BLK + YOFF
                            c = hq * Q4 * L + blk
                            for pq, pe_ in TPROD:
                                m = nc.tensor.matmul(ps[:, g * Q4 * BLK:(g + 1) * Q4 * BLK], toep[:, kind, pe_, y:y + P],
                                                     bq[:, s, pq, c:c + (Q4 * BLK - 1) * NBLK + 1:NBLK], start=False, stop=True,
                                                     skip_group_check=True)
                    m.then_inc(b_full, 1)

                def values(n, q, r, s):
                    hq, rt = r // LT, r % LT
                    if rt == 0:
                        pe.wait_ge(o_free, q + 1)
                    pe.wait_ge(e_done, 2 * n + 4)
                    p = prob[:, r % 2].rearrange("p (g h j) -> p g h j", h=Q4, j=BLK)
                    for h in range(Q4):
                        m = nc.tensor.matmul(ps_o[32 * h:32 * h + 32], vt[:, s, rt, hq * Q4 + h], p[:, :, h],
                                             start=(rt == 0), stop=(rt == LT - 1))
                    m.then_inc(p_free, 1)

                def max_rows(i, n, s):
                    pe.wait_ge(a_free, NBLK * (n + 1) + 2)
                    pe.wait_ge(m_free, i + 1)
                    nc.tensor.transpose(ps_m[0:NBLK, 0:P], mcol[:, s], ident[:]).then_inc(m_full, 1)

                def denominators(i, n, q):
                    pe.wait_ge(o_free, n + 2)
                    pe.wait_ge(m_free, i + 1)
                    nc.tensor.matmul(ps_m[:], den_sel[:], osb[:, q], start=True, stop=True).then_inc(m_full, 1)

                def output(i, b):
                    pe.wait_ge(o_done, 4 * b + 4)
                    pe.wait_ge(r_free, INNER * b + INNER + 2)
                    pe.wait_ge(m_free, i + 1)
                    for lt in range(LT):
                        ps = ps_m[:, lt * P:(lt + 1) * P]
                        for q in range(NH // Q4):
                            nc.tensor.matmul(ps, osb[:, q, lt * P:(lt + 1) * P], wo_pad[:, q], start=(lt == 0 and q == 0), stop=True,
                                             skip_group_check=True)
                        c = lt % 2 * P
                        m = nc.tensor.matmul(ps, acc[:, 1, c:c + P], wout2[:, lt // 2], start=False, stop=True, skip_group_check=True)
                    m.then_inc(m_full, 1)

                def body(b, last):
                    for hg in range(NG):
                        n = 2 * b + hg
                        pe.wait_ge(d_b[hg], 16 * NDB * (b + 1))
                        pe.wait_ge(d_m[hg], 16 * (b + 1))
                        ahead = not (last and hg == 1)
                        if ahead:
                            pe.wait_ge(d_a[1 - hg], 16 * NDA * (b + hg + 1))
                        for u in range(NU):
                            if ahead:
                                for g in range(APU * u, min(APU * u + APU, NBLK)):
                                    a_unit(NBLK * (n + 1) + g, g, 1 - hg)
                            b_unit(NU * n + u, u, hg)
                            r = NP * n + u // 2
                            if u % 2 == 0 and u >= 2:
                                values(r - 1, NQ * n + (u // 2 - 1) // LT, u // 2 - 1, hg)
                            if u == 0 and hg == 1:
                                values(r - 1, NQ * n - 1, NP - 1, 0)
                            if u == 2 and hg == 1:
                                denominators(misc(b, 2, last), 4 * b + 1, 1)
                            if u == 10:
                                denominators(misc(b, 3 * hg, last), 4 * b + 2 * hg, 2 * hg)
                            if u == 12 and ahead:
                                max_rows(misc(b, 1 + 3 * hg, last), n + 1, 1 - hg)
                    values(NP * (2 * b + 2) - 1, NQ * (2 * b + 2) - 1, NP - 1, 1)
                    denominators(misc(b, 5, last), 4 * b + 3, 3)
                    output(misc(b, 6, last), b)

                pe.wait_ge(s_ones, 17)
                pe.wait_ge(d_a[0], 16 * NDA)
                for g in range(NBLK):
                    a_unit(g, g, 0)
                max_rows(0, 0, 0)
                with pe.Fori(0, B - 1) as b:
                    body(b, False)
                body(B - 1, True)

            @block.vector
            def _(dve):
                def maximum(a, g, s):
                    dve.wait_ge(a_full, a + 1)
                    nc.vector.tensor_reduce(mcol[:, s, g:g + 1], ps_a[:, g % 2], AX_X, ALU.max, negate=True).then_inc(a_free, 1)

                def max_rows(i, n, s):
                    dve.wait_ge(m_full, i + 1)
                    nc.vector.tensor_copy(mrow[:, s], ps_m[0:NBLK, 0:P]).then_inc(m_free, 1)
                    dve.wait_ge(m_free, i + 2)
                    dve.sem_inc(mr_done, 1)

                def sums(n, q):
                    dve.wait_ge(p_free, LT * (n + 1) + 2)
                    nc.vector.tensor_copy(osb[:, q], ps_o[:]).then_inc(o_free, 1)

                def divide(i, n, q):
                    dve.wait_ge(m_full, i + 1)
                    nc.vector.reciprocal(rden[:], ps_m[:]).then_inc(m_free, 1)
                    dve.wait_ge(m_free, i + 2)
                    nc.vector.tensor_tensor(osb[:, q], osb[:, q], rden[:], ALU.mult).then_inc(o_done, 1)

                def unit_sum(b, k):
                    n = INNER * b + k
                    dve.wait_ge(r_full, n + 1)
                    if k == 0:
                        nc.vector.tensor_scalar(acc[:, 0], relu[:, 0], t["w2c"][:, 0:1], t["b2c"][:, 0:1], ALU.mult,
                                                ALU.add).then_inc(r_free, 1)
                    else:
                        dve.wait_ge(r_free, n + 2)
                        nc.vector.scalar_tensor_tensor(out=acc[:, k % 2], in0=relu[:, k % 2], scalar=t["w2c"][:, k:k + 1],
                                                       in1=acc[:, 1 - k % 2], op0=ALU.mult, op1=ALU.add).then_inc(r_free, 1)

                def body(b, last):
                    for hg in range(NG):
                        n = 2 * b + hg
                        ahead = not (last and hg == 1)
                        for u in range(NU):
                            if ahead:
                                for g in range(APU * u, min(APU * u + APU, NBLK)):
                                    maximum(NBLK * (n + 1) + g, g, 1 - hg)
                            if u % 2 == 1:
                                unit_sum(b, (NU * hg + u) // 2)
                            if u == 1 and hg == 1:
                                sums(4 * b + 1, 1)
                            if u == 3 and hg == 1:
                                divide(misc(b, 2, last), 4 * b + 1, 1)
                            if u == 9:
                                sums(4 * b + 2 * hg, 2 * hg)
                            if u == 11:
                                divide(misc(b, 3 * hg, last), 4 * b + 2 * hg, 2 * hg)
                            if u == 13 and ahead:
                                max_rows(misc(b, 1 + 3 * hg, last), n + 1, 1 - hg)
                    sums(4 * b + 3, 3)
                    divide(misc(b, 5, last), 4 * b + 3, 3)
                    dve.wait_ge(m_full, misc(b, 6, last) + 1)
                    nc.vector.tensor_tensor(base[:, b], base[:, b], ps_m[:].rearrange("p (n f) -> p n f", n=LT),
                                            ALU.add).then_inc(m_free, 1)
                    dve.wait_ge(m_free, misc(b, 6, last) + 2)
                    dve.sem_inc(s_res, 1)

                dve.sem_inc(a_free, 2)
                dve.sem_inc(o_free, 1)
                dve.sem_inc(m_free, 1)
                dve.sem_inc(r_free, 2)
                nc.vector.memset(ones[:], 1.0).then_inc(s_ones, 1)
                nc.vector.memset(bq[:, 0].bitcast(F32), 0.0).then_inc(s_zero, 1)
                nc.vector.memset(bq[:, 1].bitcast(F32), 0.0).then_inc(s_zero, 1)
                for g in range(NBLK):
                    maximum(g, g, 0)
                max_rows(0, 0, 0)
                with dve.Fori(0, B - 1) as b:
                    body(b, False)
                body(B - 1, True)

            @block.scalar
            def _(act):
                act.sem_inc(e_done, 2)
                act.sem_inc(p_free, 2)

                def body(b):
                    for u in range(2 * NU):
                        n = 2 * NU * b + u
                        act.wait_ge(b_full, n + 1)
                        if u % 2 == 0:
                            act.wait_ge(p_free, NU * b + u // 2 + 1)
                        nc.scalar.activation(prob[:, u // 2 % 2, u % 2 * 2 * L:(u % 2 + 1) * 2 * L], ps_b[:, u % 2],
                                             ACT.Exp).then_inc(e_done, 1)
                        if u % 2 == 0:
                            k = u // 2
                            if k == 0:
                                nc.scalar.copy(s_cur[:], s_all[:, b]).then_inc(s_cp, 1)
                            act.wait_ge(s_cp, b + 1)
                            act.wait_ge(r_free, INNER * b + k + 1)
                            nc.scalar.activation(relu[:, k % 2], s_cur[:], ACT.Relu, bias=t["b1c"][:, k:k + 1],
                                                 scale=t["w1c"][:, k:k + 1]).then_inc(r_full, 1)

                with act.Fori(0, B) as b:
                    body(b)


_INS = ["L0_attn_hidden_states", "L0_attn_Wq", "L0_attn_bq", "L0_attn_Wk", "L0_attn_bk", "L0_attn_Wv", "L0_attn_bv",
        "L0_attn_Wo", "L0_attn_bo", "L0_attn_dist_emb", "L0_ffn_Win", "L0_ffn_bin_", "L0_ffn_W1", "L0_ffn_b1",
        "L0_ffn_W2", "L0_ffn_b2", "L0_ffn_Wout", "L0_ffn_bout"]


def kernel(**inputs):
    import numpy as _np
    import concourse.bacc as _bacc
    from concourse import mybir as _mybir
    from concourse.bass_utils import run_bass_kernel_spmd as _run

    nc = _bacc.Bacc("TRN2", target_bir_lowering=False, num_devices=1)
    arrays, args = {}, []
    for name in _INS:
        a = _np.ascontiguousarray(inputs[name])
        arrays[f"in_{name}_dram"] = a
        args.append(nc.dram_tensor(f"in_{name}_dram", a.shape, _mybir.dt.from_np(a.dtype), kind="ExternalInput").ap())
    args.append(nc.dram_tensor("out_0_dram", (B, L, H), _mybir.dt.from_np(_np.dtype("float32")), kind="ExternalOutput").ap())
    build(nc, *args)
    r = _run(nc, [arrays], core_ids=[0])
    return r.results[0]["out_0_dram"]
```

```python
from contextlib import ExitStack

import concourse.bass as bass
from concourse import mybir

F32 = mybir.dt.float32
BF16 = mybir.dt.bfloat16
F16 = mybir.dt.float16
ALU = mybir.AluOpType
ACT = mybir.ActivationFunctionType
AX_X = mybir.AxisListType.X

B, L, H = 8, 512, 128
NH, D = 16, 8
LEFT, RIGHT = 64, 8
NPOS = LEFT + RIGHT + 1
M, INNER = 64, 16
P = 128
LT = L // P
BLK = P // D
NBLK = L // BLK
G = 8
NG = NH // G
Q4 = 4
NQ = G // Q4
LN_EPS = 1e-5
SCALE = float(D) ** -0.5
PROD = [(0, 0), (0, 1), (0, 2), (1, 0), (1, 1), (2, 0)]
KROWS = len(PROD) * D
MROW = KROWS
K_MID, K_LEFT, K_RIGHT = range(3)
LW = L - BLK - LEFT
RBEG = BLK + RIGHT
KW = LW + L + (L - RBEG)
KPOS = (LW, 0, LW + L - RBEG)
VW = 16
YOFF = P + LEFT - BLK
YLEN = YOFF + P + BLK
XOFF = YOFF + BLK - 1
XLEN = YLEN + BLK - 1
TPROD = [(0, 0), (0, 1), (1, 0)]


def tile_kind(rt, lt):
    return K_MID if rt == lt else K_RIGHT if lt < rt else K_LEFT


def mixed_blocks(rt, lt):
    out = []
    for g in range(P // BLK):
        d0 = (lt - rt) * P + g * BLK
        right = -d0 - (BLK - 1) >= RIGHT
        left = P - 1 - d0 <= -LEFT
        if not (right or left):
            out.append(g)
    return out


def build(nc, hidden, Wq, bq, Wk, bk, Wv, bv, Wo, bo, emb, Win, bin_, W1, b1, W2, b2, Wout, bout, out):
    qk_d = nc.dram_tensor("qk_parts", [3, P, B, L + KW], BF16, kind="Internal").ap()
    qd_d = nc.dram_tensor("q_blocked", [P, B, BLK, NBLK], BF16, kind="Internal").ap()
    qc_d = nc.dram_tensor("q_half_parts", [NG, B, BLK, D, G, 2, NBLK], F16, kind="Internal").ap()
    v_d = nc.dram_tensor("v_rows", [P, B, LT, NH, VW], F32, kind="Internal").ap()
    m_d = nc.dram_tensor("max_rows", [2, G, NBLK, BLK], BF16, kind="Internal").ap()
    x_t = hidden.rearrange("b (t p) f -> p b t f", p=P)
    o_t = out.rearrange("b (t p) f -> p b t f", p=P)

    with ExitStack() as whole:
        def sb(ctx, name, shape, dt):
            return ctx.enter_context(nc.sbuf_tensor(name, shape, dt))

        base = sb(whole, "base", [P, B, LT, H], F32)
        s_all = sb(whole, "s_all", [P, B, L // 2], F32)
        ident = sb(whole, "ident", [P, P], F32)
        toep = sb(whole, "toep", [P, 3, 2, YLEN], F16)
        wo_t = sb(whole, "wo_t", [P, H], F32)
        wout2 = sb(whole, "wout2", [P, 2, H], F32)
        mask_f = sb(whole, "mask_f", [P, BLK], F32)
        mask_h = sb(whole, "mask_h", [P, BLK], F16)
        mask_b = sb(whole, "mask_b", [P, BLK], BF16)
        w1c = sb(whole, "w1c", [P, INNER], F32)
        b1c = sb(whole, "b1c", [P, INNER], F32)
        w2c = sb(whole, "w2c", [P, INNER], F32)
        b2c = sb(whole, "b2c", [P, 1], F32)

        prepare(nc, sb, locals())
        attend(nc, sb, locals())


def prepare(nc, sb, t):
    x_t, base, s_all, ident, toep = t["x_t"], t["base"], t["s_all"], t["ident"], t["toep"]
    wout2, mask_f, mask_h, mask_b = t["wout2"], t["mask_f"], t["mask_h"], t["mask_b"]
    with ExitStack() as ctx:
        def pb(name, shape, dt=F32):
            return ctx.enter_context(nc.psum_tensor(name, shape, dt))

        def sem(name):
            return ctx.enter_context(nc.semaphore(name))

        wraw = sb(ctx, "wraw", [P, 4, H], F32)
        wT = sb(ctx, "wT", [P, 3, H], F32)
        win = sb(ctx, "win", [P, M], F32)
        colb = sb(ctx, "colb", [P, 8], F32)
        colc = sb(ctx, "colc", [P, 4], F32)
        rows = sb(ctx, "rows", [P, 4, H], F32)
        emb_sb = sb(ctx, "emb_sb", [P, D], F32)
        ep = sb(ctx, "ep", [D, 3, XLEN], F32)
        eph = sb(ctx, "eph", [D, 3, 2, XLEN], F16)
        xn = sb(ctx, "xn", [P, 2, LT, H], F32)
        xT = sb(ctx, "xT", [P, 2, L], F32)
        stats = sb(ctx, "stats", [P, B, LT, 6], F32)
        mv = sb(ctx, "mv", [P, B, LT, 2], F32)
        var = sb(ctx, "var", [P, B, LT], F32)
        std = sb(ctx, "std", [P, B, LT], F32)
        rs0 = sb(ctx, "rs0", [P, B, LT], F32)
        tmp = sb(ctx, "tmp", [P, 2, B, LT], F32)
        rstd = sb(ctx, "rstd", [P, B, LT], F32)
        qkf = sb(ctx, "qkf", [P, 2, L + KW], F32)
        rem = sb(ctx, "rem", [P, 2, L + KW], F32)
        parts = sb(ctx, "parts", [P, 2, 3, L + KW], BF16)
        qd = sb(ctx, "qd", [P, 2, BLK, NBLK], BF16)
        qh = sb(ctx, "qh", [P, 2, BLK, 2, NBLK], F16)
        vrow = sb(ctx, "vrow", [P, 2, LT, NH, VW], F32)

        ps_t = pb("ps_t", [P, 2, L])
        ps_q = pb("ps_q", [P, L])
        ps_k = pb("ps_k", [P, L])
        ps_v = pb("ps_v", [P, 2, L])
        ps_s = pb("ps_s", [P, L])
        ps_w = pb("ps_w", [P, L])

        c_x = [sem(f"c_x{i}") for i in range(B // 2)]
        c_w, c_cst, c_pad, c_out = sem("c_w"), sem("c_cst"), sem("c_pad"), [sem("c_out0"), sem("c_out1")]
        c_zero, c_ident = sem("c_zero"), sem("c_ident")
        c_wT, c_wTc = sem("c_wT"), sem("c_wTc")
        c_ebT, c_ep = sem("c_ebT"), sem("c_ep")
        c_col, c_row, c_vec, c_var = sem("c_col"), sem("c_row"), sem("c_vec"), sem("c_var")
        c_ln, c_t, c_tc = sem("c_ln"), sem("c_t"), sem("c_tc")
        c_qk, c_v, c_s = sem("c_qk"), sem("c_v"), sem("c_s")
        c_qkf, c_sc, c_vc = sem("c_qkf"), sem("c_sc"), sem("c_vc")
        c_hi, c_hb, c_rem, c_mid, c_lo, c_ql = (sem(n) for n in ("c_hi", "c_hb", "c_rem", "c_mid", "c_lo", "c_ql"))
        c_base = sem("c_base")
        NW, NCST, NPAD = 5, 9, 8
        NST = 16 * (3 + NH)

        with nc.Block() as block:
            @block.sync
            def _(sp):
                for n, w in enumerate(("Wq", "Wk", "Wv", "Wo")):
                    sp.dma_start(wraw[:, n], t[w]).then_inc(c_w, 16)
                sp.dma_start(emb_sb[0:NPOS, :], t["emb"]).then_inc(c_w, 16)
                for b in range(B):
                    sp.dma_start(base[:, b], x_t[:, b]).then_inc(c_x[b // 2], 16)

                def on_rows(v, n):
                    return bass.AP(v.tensor, v.offset, [[0, n], [1, H]])

                sp.dma_start(win[:], t["Win"]).then_inc(c_cst, 16)
                sp.dma_start(colb[:, 0:1], t["bq"].rearrange("(p a) -> p a", a=1)).then_inc(c_cst, 16)
                sp.dma_start(colb[:, 1:2], t["bk"].rearrange("(p a) -> p a", a=1)).then_inc(c_cst, 16)
                for n, row in ((2, 0), (3, NPOS - 1)):
                    e = t["emb"][row]
                    sp.dma_start(colb[:, n:n + 1], bass.AP(e.tensor, e.offset, [[0, NH], [1, D], [1, 1]])).then_inc(c_cst, 16)
                for n, v in enumerate(("bv", "bo", "bout")):
                    sp.dma_start(rows[:, n], on_rows(t[v], P)).then_inc(c_row, 16)
                for h in range(2):
                    half = slice(M * h, M * h + M)
                    sp.dma_start(colb[half, 4:5], t["bin_"].rearrange("(p a) -> p a", a=1)).then_inc(c_row, 16)
                    sp.dma_start(t["b2c"][half], t["b2"].rearrange("(p a) -> p a", a=1)).then_inc(c_pad, 16)
                    sp.dma_start(t["w1c"][half], t["W1"]).then_inc(c_pad, 16)
                    sp.dma_start(t["b1c"][half], t["b1"]).then_inc(c_pad, 16)
                    sp.dma_start(t["w2c"][half], t["W2"]).then_inc(c_pad, 16)

                def store(b, s):
                    sp.wait_ge(c_hb, 3 * b + 3)
                    sp.dma_start(t["qd_d"][:, b], qd[:, s]).then_inc(c_out[s], 16)
                    sp.wait_ge(c_ql, b + 1)
                    for h in range(NH):
                        sp.dma_start(t["qc_d"][h // G, b, :, :, h % G].rearrange("j d a g -> d j (a g)"),
                                     qh[h * D:(h + 1) * D, s].rearrange("d j a g -> d j (a g)")).then_inc(c_out[s], 16)
                    sp.wait_ge(c_vc, b + 3)
                    sp.dma_start(t["v_d"][:, b], vrow[:, s]).then_inc(c_out[s], 16)
                    sp.wait_ge(c_lo, b + 1)
                    sp.dma_start(t["qk_d"][:, :, b].rearrange("a p l -> p a l"), parts[:, s]).then_inc(c_out[s], 16)

                store(0, 0)
                sp.wait_ge(c_ep, 3)
                for j in range(BLK):
                    sp.dma_start(toep[j * D:(j + 1) * D], eph[:, :, :, BLK - 1 - j:BLK - 1 - j + YLEN]).then_inc(c_pad, 16)
                sp.wait_ge(c_zero, 3)
                for h in range(2):
                    sp.dma_start(wout2[M * h:M * h + M, h], t["Wout"]).then_inc(c_pad, 16)
                store(1, 1)
                with sp.Fori(1, B // 2) as i:
                    for s in range(2):
                        store(2 * i + s, s)
                sp.wait_ge(c_pad, 16 * (NPAD + BLK + 2))
                for s in range(2):
                    sp.wait_ge(c_out[s], NST * (B // 2) + 1)

            @block.gpsimd
            def _(pool):
                nc.gpsimd.memset(ident[:], 0.0).then_inc(c_zero, 1)
                nc.gpsimd.memset(mask_f[:], 1.0).then_inc(c_zero, 1)
                nc.gpsimd.memset(wout2[:], 0.0).then_inc(c_zero, 1)
                pool.wait_ge(c_zero, 3)
                nc.gpsimd.affine_select(out=ident[:], in_=ident[:], compare_op=ALU.not_equal, fill=1.0, base=0,
                                        pattern=[[-1, P]], channel_multiplier=1).then_inc(c_ident, 1)
                nc.gpsimd.affine_select(out=mask_f[:], in_=mask_f[:], compare_op=ALU.is_ge, fill=0.0, base=0,
                                        pattern=[[-D, BLK]], channel_multiplier=1).then_inc(c_ident, 1)
                pool.wait_ge(c_ident, 2)
                nc.gpsimd.affine_select(out=mask_f[:], in_=mask_f[:], compare_op=ALU.is_ge, fill=0.0, base=D - 1,
                                        pattern=[[D, BLK]], channel_multiplier=-1).then_inc(c_ident, 1)
                pool.wait_ge(c_ident, 3)
                nc.gpsimd.tensor_copy(mask_h[:], mask_f[:]).then_inc(c_ident, 1)
                nc.gpsimd.tensor_copy(mask_b[:], mask_f[:]).then_inc(c_ident, 1)
                pool.wait_ge(c_row, 16 * 5 + 1)
                with pool.Fori(0, B // 2) as i:
                    for s in range(2):
                        b = 2 * i + s
                        pool.wait_ge(c_ln, b + 1)
                        nc.gpsimd.tensor_tensor(base[:, b], base[:, b], rows[:, 3:4].broadcast_to([P, LT, H]), ALU.add).then_inc(c_base, 1)
                        pool.wait_ge(c_mid, b + 1)
                        nc.gpsimd.tensor_tensor(parts[:, s, 2], rem[:, s], parts[:, s, 1], ALU.subtract).then_inc(c_lo, 1)

            @block.tensor
            def _(pe):
                pe.wait_ge(c_w, 16 * NW)
                pe.wait_ge(c_ident, 1)
                for n in range(4):
                    w = nc.tensor.transpose(ps_w[:, n * H:(n + 1) * H], wraw[:, n], ident[:])
                w.then_inc(c_wT, 1)
                nc.tensor.transpose(ps_s[0:D, 0:NPOS], emb_sb[0:NPOS, :], ident[0:NPOS, 0:NPOS]).then_inc(c_ebT, 1)
                pe.wait_ge(c_wTc, 1)
                pe.wait_ge(c_ep, 1)
                pe.wait_ge(c_cst, 16 * 5)
                with pe.Fori(0, B // 2) as i:
                    for s in range(2):
                        b = 2 * i + s
                        pe.wait_ge(c_ln, b + 1)
                        pe.wait_ge(c_tc, b + 1)
                        for n in range(LT):
                            m = nc.tensor.transpose(ps_t[:, s, n * P:(n + 1) * P], xn[:, s, n], ident[:])
                        m.then_inc(c_t, 1)
                        pe.wait_ge(c_tc, b + 2)
                        pe.wait_ge(c_qkf, 4 * b + 1)
                        nc.tensor.matmul(ps_q[:], wT[:, 0], xT[:, s], start=True, stop=True).then_inc(c_qk, 1)
                        nc.tensor.matmul(ps_k[:], wT[:, 1], xT[:, s], start=True, stop=True).then_inc(c_qk, 1)
                        pe.wait_ge(c_vc, b + 1)
                        for n in range(LT):
                            m = nc.tensor.matmul(ps_v[:, s, n * P:(n + 1) * P], xT[:, s, n * P:(n + 1) * P], wT[:, 2],
                                                 start=(n == 0), stop=True, skip_group_check=True)
                        m.then_inc(c_v, 1)
                        pe.wait_ge(c_sc, b + 1)
                        for h in range(2):
                            m = nc.tensor.matmul(ps_s[M * h:M * h + M, 0:L // 2], win[:], xT[:, s, h * (L // 2):(h + 1) * (L // 2)],
                                                 start=True, stop=True)
                        m.then_inc(c_s, 1)

            @block.vector
            def _(dve):
                cnt = [0]

                def link(ins):
                    cnt[0] += 1
                    ins.then_inc(c_vec, 1)
                    dve.wait_ge(c_vec, cnt[0])

                def normal(b, s):
                    for n in range(LT):
                        m = nc.vector.tensor_scalar(xn[:, s, n], base[:, b, n], mv[:, b, n, 0:1], rstd[:, b, n:n + 1],
                                                    ALU.subtract, ALU.mult)
                    m.then_inc(c_ln, 1)

                def turned(b, s):
                    dve.wait_ge(c_t, b + 1)
                    nc.vector.tensor_copy(xT[:, s], ps_t[:, s]).then_inc(c_tc, 1)

                def body(i, last):
                    for s in range(2):
                        b = 2 * i + s
                        ahead = not (last and s == 1)
                        if ahead:
                            dve.wait_ge(c_t, b + 1)
                            normal(b + 1, 1 - s)
                        dve.wait_ge(c_hi, b + 1)
                        nc.vector.tensor_tensor(rem[:, s], qkf[:, s], parts[:, s, 0], ALU.subtract).then_inc(c_rem, 1)
                        if ahead:
                            dve.wait_ge(c_s, b + 1)
                            turned(b + 1, 1 - s)
                        dve.wait_ge(c_hb, 3 * b + 3)
                        nc.vector.tensor_tensor(qh[:, s, :, 1].rearrange("p j g -> p g j"),
                                                qkf[:, s, 0:L].rearrange("p (g j) -> p g j", j=BLK),
                                                qh[:, s, :, 0].rearrange("p j g -> p g j"), ALU.subtract).then_inc(c_ql, 1)
                        dve.wait_ge(c_s, b + 1)
                        nc.vector.tensor_scalar(s_all[:, b], ps_s[:, 0:L // 2], colb[:, 4:5], None, ALU.add).then_inc(c_sc, 1)
                        dve.wait_ge(c_v, b + 1)
                        dve.wait_ge(c_out[s], NST * i + 1)
                        nc.vector.tensor_tensor(vrow[:, s, :, :, 0:D], ps_v[:, s].rearrange("p (n h d) -> p n h d", n=LT, h=NH),
                                                rows[:, 0:1].broadcast_to([P, LT, H]).rearrange("p n (h d) -> p n h d", h=NH),
                                                ALU.add).then_inc(c_vc, 1)

                dve.sem_inc(c_tc, 1)
                dve.sem_inc(c_sc, 1)
                dve.sem_inc(c_vc, 2)
                link(nc.vector.memset(vrow[:], 0.0))
                link(nc.vector.memset(vrow[:, :, :, :, D:D + 1], 1.0))
                link(nc.vector.memset(ep[:, 0], 0.0))
                dve.wait_ge(c_wT, 1)
                nc.vector.tensor_copy(wT[:].rearrange("p n f -> p (n f)"), ps_w[:, 0:3 * H]).then_inc(c_wTc, 1)
                nc.vector.tensor_copy(t["wo_t"][:], ps_w[:, 3 * H:4 * H]).then_inc(c_wTc, 1)
                band0 = XOFF - LEFT
                dve.wait_ge(c_ebT, 1)
                nc.vector.tensor_copy(ep[:, 0, band0:band0 + NPOS], ps_s[0:D, 0:NPOS]).then_inc(c_ep, 1)
                for b in range(B):
                    if b % 2 == 0:
                        dve.wait_ge(c_x[b // 2], 32)
                    for n in range(LT):
                        m = nc.vector.bn_stats(stats[:, b, n], base[:, b, n])
                link(m)
                for b in range(B):
                    for n in range(LT):
                        m = nc.vector.bn_aggr(mv[:, b, n], stats[:, b, n])
                link(m)
                nc.vector.tensor_scalar(var[:], mv[:, :, :, 1], LN_EPS, None, ALU.add).then_inc(c_var, 1)
                dve.wait_ge(c_cst, 16 * 5)
                nc.vector.tensor_scalar(colc[:, 0:1], colb[:, 0:1], SCALE, None, ALU.mult).then_inc(c_col, 1)
                nc.vector.tensor_copy(colc[:, 1:2], colb[:, 1:2]).then_inc(c_col, 1)
                nc.vector.tensor_tensor(colc[:, 2:3], colb[:, 1:2], colb[:, 2:3], ALU.add).then_inc(c_col, 1)
                nc.vector.tensor_tensor(colc[:, 3:4], colb[:, 1:2], colb[:, 3:4], ALU.add).then_inc(c_col, 1)
                dve.wait_ge(c_var, 2)
                link(nc.vector.reciprocal(rs0[:], std[:]))
                link(nc.vector.tensor_tensor(tmp[:, 0], rs0[:], rs0[:], ALU.mult))
                link(nc.vector.tensor_tensor(tmp[:, 1], tmp[:, 0], var[:], ALU.mult))
                link(nc.vector.tensor_scalar(tmp[:, 0], tmp[:, 1], -0.5, 1.5, ALU.mult, ALU.add))
                link(nc.vector.tensor_tensor(rstd[:], rs0[:], tmp[:, 0], ALU.mult))
                normal(0, 0)
                dve.wait_ge(c_row, 16 * 5)
                nc.vector.tensor_tensor(rows[:, 3], rows[:, 1], rows[:, 2], ALU.add).then_inc(c_row, 1)
                turned(0, 0)
                e_l, e_r = ep[:, 0, band0:band0 + 1], ep[:, 0, band0 + NPOS - 1:band0 + NPOS]
                link(nc.vector.tensor_scalar(ep[:, 0, 0:band0], ep[:, 0, 0:band0], e_l, None, ALU.add))
                link(nc.vector.tensor_scalar(ep[:, 0, band0 + NPOS:XLEN], ep[:, 0, band0 + NPOS:XLEN], e_r, None, ALU.add))
                link(nc.vector.tensor_scalar(ep[:, K_LEFT], ep[:, 0], e_l, None, ALU.subtract))
                link(nc.vector.tensor_scalar(ep[:, K_RIGHT], ep[:, 0], e_r, None, ALU.subtract))
                nc.vector.tensor_copy(eph[:, :, 0], ep[:]).then_inc(c_ep, 1)
                dve.wait_ge(c_ep, 2)
                nc.vector.tensor_tensor(eph[:, :, 1], ep[:], eph[:, :, 0], ALU.subtract).then_inc(c_ep, 1)
                with dve.Fori(0, B // 2 - 1) as i:
                    body(i, False)
                body(B // 2 - 1, True)

            @block.scalar
            def _(act):
                act.sem_inc(c_qkf, 1)
                for s in range(2):
                    act.sem_inc(c_out[s], 1)
                act.wait_ge(c_var, 1)
                nc.scalar.activation(std[:], var[:], ACT.Sqrt).then_inc(c_var, 1)
                act.wait_ge(c_col, 4)
                with act.Fori(0, B // 2) as i:
                    for s in range(2):
                        b = 2 * i + s
                        act.wait_ge(c_qk, 2 * b + 1)
                        act.wait_ge(c_vc, b + 1)
                        act.wait_ge(c_out[s], NST * i + 1)
                        nc.scalar.activation(qkf[:, s, 0:L], ps_q[:], ACT.Identity, bias=colc[:, 0:1], scale=SCALE).then_inc(c_qkf, 1)
                        act.wait_ge(c_qk, 2 * b + 2)
                        for kind, r0, r1 in ((K_LEFT, 0, LW), (K_MID, 0, L), (K_RIGHT, RBEG, L)):
                            o = L + KPOS[kind]
                            nc.scalar.activation(qkf[:, s, o + r0:o + r1], ps_k[:, r0:r1], ACT.Identity,
                                                 bias=colc[:, 1 + kind:2 + kind], scale=1.0).then_inc(c_qkf, 1)
                        act.wait_ge(c_qkf, 4 * b + 5)
                        nc.scalar.copy(parts[:, s, 0], qkf[:, s]).then_inc(c_hi, 1)
                        blocked = qkf[:, s, 0:L].rearrange("p (g j) -> p j g", j=BLK)
                        nc.scalar.copy(qd[:, s], blocked).then_inc(c_hb, 1)
                        nc.scalar.copy(qh[:, s, :, 0], blocked).then_inc(c_hb, 2)
                        act.wait_ge(c_rem, b + 1)
                        nc.scalar.copy(parts[:, s, 1], rem[:, s]).then_inc(c_mid, 1)


def attend(nc, sb, t):
    base, s_all, ident, toep = t["base"], t["s_all"], t["ident"], t["toep"]
    wo_t, wout2, mask_h, mask_b = t["wo_t"], t["wout2"], t["mask_h"], t["mask_b"]
    with ExitStack() as ctx:
        def pb(name, shape, dt=F32):
            return ctx.enter_context(nc.psum_tensor(name, shape, dt))

        def sem(name):
            return ctx.enter_context(nc.semaphore(name))

        qst = sb(ctx, "qst", [KROWS + 1, 2, G, L], BF16)
        kst = sb(ctx, "kst", [KROWS + 1, 2, G, KW], BF16)
        vt = sb(ctx, "vt", [P, 2, LT, G, VW], F32)
        qc = sb(ctx, "qc", [P, 2, G, 2, NBLK], F16)
        bq = sb(ctx, "bq", [P, 2, 2, G, BLK, NBLK], F16)
        bqa = sb(ctx, "bqa", [P, 2, G, BLK, NBLK], F16)
        qx = sb(ctx, "qx", [G * D, 2, L], BF16)
        bd = sb(ctx, "bd", [G * D, 2, G, L], BF16)
        ka = sb(ctx, "ka", [G * D, 2, KW], BF16)
        prob = sb(ctx, "prob", [P, 2, LT * (P // BLK) * Q4 * BLK], F32)
        osb = sb(ctx, "osb", [P, 2, L], F32)
        rden = sb(ctx, "rden", [P, 2, LT, Q4], F32)
        onorm = sb(ctx, "onorm", [P, LT, NH // Q4, Q4, D], F32)
        oT = sb(ctx, "oT", [P, L], F32)
        s_cur = sb(ctx, "s_cur", [P, L // 2], F32)
        relu = sb(ctx, "relu", [P, 2, L // 2], F32)
        acc = sb(ctx, "acc", [P, 2, L // 2], F32)
        gT = sb(ctx, "gT", [P, L // 2], F32)
        mcol = sb(ctx, "mcol", [P, 2, NBLK], F32)
        mrow = sb(ctx, "mrow", [NBLK, 2, P], BF16)

        ps_a = pb("ps_a", [P, 2, L])
        ps_b = pb("ps_b", [P, 2, 2 * L])
        ps_o = pb("ps_o", [P, L])
        ps_m = pb("ps_m", [P, L])

        d_q, d_k, d_b, d_m = ([sem(f"{n}{s}") for s in range(2)] for n in ("d_q", "d_k", "d_b", "d_m"))
        s_cp, d_md = sem("s_cp"), sem("d_md")
        s_ones, s_zero = sem("s_ones"), sem("s_zero")
        g_a, g_hi, g_lo = sem("g_a"), sem("g_hi"), sem("g_lo")
        a_full, a_free = sem("a_full"), sem("a_free")
        b_full, e_done = sem("b_full"), sem("e_done")
        p_free = sem("p_free")
        o_free = sem("o_free")
        m_full, m_free = sem("m_full"), sem("m_free")
        s_rec = sem("s_rec")
        r_full, r_free = sem("r_full"), sem("r_free")
        s_done = sem("s_done")

        NDQ = 2
        NDB = 2 * len(PROD) + 1
        NU = NQ * LT * 2
        NP = NQ * LT
        APU = NBLK // NU
        U_A = 11
        A0 = APU * (NU - U_A)
        T3, OT, OUT, T0, MAX1, T1, T2, MAX2 = range(8)
        NMISC = 8

        def misc(b, i, last=False):
            return NMISC * b + i - 2 - (1 if last and i >= NMISC else 0)

        def a_units(hg, u, first_only=False):
            if u < U_A:
                return [(1, A0 + APU * u + i) for i in range(APU)]
            return [(2, APU * (u - U_A) + i) for i in range(APU)]

        def has(n_ahead, hg, last):
            return not last or hg + n_ahead < NG

        with nc.Block() as block:
            @block.sync
            def _(sp):
                def load_q(b, hg):
                    sp.dma_start(qc[:, hg].rearrange("p h a g -> p (h a g)"),
                                 t["qc_d"][hg, b].rearrange("j d h a g -> (j d) (h a g)")).then_inc(d_q[hg], 16)
                    sp.dma_start(qx[:, hg], t["qd_d"][hg * G * D:(hg + 1) * G * D, b].rearrange("p j g -> p (j g)")).then_inc(d_q[hg], 16)

                def load_k(b, hg):
                    sp.dma_start(ka[:, hg], t["qk_d"][0, hg * G * D:(hg + 1) * G * D, b, L:]).then_inc(d_k[hg], 16)

                def load_b(b, hg):
                    hd = slice(hg * G * D, (hg + 1) * G * D)
                    for n, (pq, pk) in enumerate(PROD):
                        r = slice(n * D, (n + 1) * D)
                        for dst, src in ((qst[r, hg], t["qk_d"][pq, hd, b, 0:L]), (kst[r, hg], t["qk_d"][pk, hd, b, L:])):
                            sp.dma_start(dst, src.rearrange("(h d) l -> d h l", h=G)).then_inc(d_b[hg], 16)

                def load_v(b, hg):
                    sp.dma_start(vt[:, hg], t["v_d"][:, b, :, hg * G:(hg + 1) * G]).then_inc(d_b[hg], 16)

                def max_row(n, s, i):
                    sp.wait_ge(m_free, i + 2)
                    sp.dma_start(t["m_d"][s].rearrange("h g j -> g h j"), mrow[:, s].rearrange("g (h j) -> g h j", h=G)).then_inc(d_md, 16)
                    sp.wait_ge(d_md, 16 * (n + 1))
                    sp.dma_start(qst[MROW:MROW + 1, s], t["m_d"][s].rearrange("h g j -> (h g j)").rearrange("(a h l) -> a h l", a=1, h=G)).then_inc(d_m[s], 16)

                def store(b, i):
                    sp.wait_ge(m_free, i + 2)
                    sp.dma_start(t["o_t"][:, b], base[:, b]).then_inc(s_done, 16)

                def body(b, first, last):
                    nxt = b + 1 if first or last else sp.snap(b + 1)
                    for hg in range(NG):
                        n = 2 * b + hg
                        o = 1 - hg
                        if has(2, hg, last):
                            sp.wait_ge(g_lo, n + 1)
                            load_q(nxt, hg)
                            sp.wait_ge(a_full, NBLK * (n + 1))
                            load_k(nxt, hg)
                        if has(1, hg, last):
                            if not (first and hg == 0):
                                sp.wait_ge(p_free, NP * n + 2)
                            load_v(nxt if hg else b, o)
                            load_b(nxt if hg else b, o)
                        if hg == 0 and not first:
                            store(b - 1, misc(b, OUT))
                        if has(1, hg, last):
                            max_row(n + 1, o, misc(b, MAX1 if hg == 0 else MAX2))

                load_q(0, 0)
                load_k(0, 0)
                load_q(0, 1)
                load_k(0, 1)
                sp.wait_ge(s_ones, 1)
                load_b(0, 0)
                load_v(0, 0)
                max_row(0, 0, 0)
                body(0, True, False)
                with sp.Fori(1, B - 1) as b:
                    body(b, False, False)
                body(B - 1, False, True)
                store(B - 1, misc(B - 1, NMISC + OUT, True))
                sp.wait_ge(s_done, 16 * B)

            @block.gpsimd
            def _(pool):
                def diagonal(s):
                    nc.gpsimd.tensor_tensor(bd[:, s], qx[:, s].unsqueeze(1).broadcast_to([G * D, G, L]),
                                            mask_b[0:G * D, 0:G].unsqueeze(2).broadcast_to([G * D, G, L]), ALU.mult).then_inc(g_a, 1)
                    spread(bqa[:, s], s, 0).then_inc(g_a, 1)

                def spread(out, s, part):
                    return nc.gpsimd.tensor_tensor(out, qc[:, s, :, part].unsqueeze(2).broadcast_to([P, G, BLK, NBLK]),
                                                   mask_h[:].unsqueeze(1).unsqueeze(3).broadcast_to([P, G, BLK, NBLK]), ALU.mult)

                def body(b, first, last):
                    for hg in range(NG):
                        n = 2 * b + hg
                        if has(2, hg, last):
                            pool.wait_ge(d_q[hg], 16 * NDQ * (b + 2))
                            pool.wait_ge(a_full, NBLK * (n + 1))
                            pool.wait_ge(g_hi, n + 1)
                            diagonal(hg)
                        if has(1, hg, last):
                            if not (first and hg == 0):
                                pool.wait_ge(b_full, NU * n)
                            spread(bq[:, 1 - hg, 1], 1 - hg, 1).then_inc(g_lo, 1)

                pool.wait_ge(d_q[0], 16 * NDQ)
                diagonal(0)
                spread(bq[:, 0, 1], 0, 1).then_inc(g_lo, 1)
                pool.wait_ge(d_q[1], 16 * NDQ)
                diagonal(1)
                body(0, True, False)
                with pool.Fori(1, B - 1) as b:
                    body(b, False, False)
                body(B - 1, False, True)

            @block.tensor
            def _(pe):
                def a_ready(b, hg):
                    pe.wait_ge(g_a, 2 * (2 * b + hg) + 2)
                    pe.wait_ge(d_k[hg], 16 * (b + 1))

                def a_unit(a, g, s):
                    ps = ps_a[:, g % 2]
                    c0, c1 = max(0, g * BLK - LEFT), min(L, g * BLK + BLK + RIGHT)
                    pe.wait_ge(a_free, a + 1)
                    first = True
                    for kind, lo, hi in ((K_LEFT, 0, c0), (K_MID, c0, c1), (K_RIGHT, c1, L)):
                        if hi > lo:
                            o = KPOS[kind]
                            nc.tensor.matmul(ps[:, lo:hi], bd[:, s].rearrange("p h (j g) -> p (h j) g", j=BLK)[:, :, g],
                                             ka[:, s, o + lo:o + hi], start=first, stop=True, skip_group_check=True)
                            first = False
                    y = c0 - g * BLK + YOFF
                    nc.tensor.matmul(ps[:, c0:c1], bqa[:, s].rearrange("p h j g -> p (h j) g")[:, :, g],
                                     toep[:, K_MID, 0, y:y + c1 - c0], start=False, stop=True, skip_group_check=True).then_inc(a_full, 1)

                def b_unit(n, u, s):
                    hq, rt, half = u // (2 * LT), u // 2 % LT, u % 2
                    pe.wait_ge(e_done, n + 1)
                    for i in range(2):
                        lt = 2 * half + i
                        kind = tile_kind(rt, lt)
                        ps = ps_b[:, u % 2, i * L:(i + 1) * L]
                        by_head = ps.rearrange("p (g h j) -> p g h j", g=P // BLK, h=Q4)
                        k0 = KPOS[kind] + rt * P
                        for h in range(Q4):
                            m = nc.tensor.matmul(by_head[:, :, h], kst[:, s, hq * Q4 + h, k0:k0 + P],
                                                 qst[:, s, hq * Q4 + h, lt * P:(lt + 1) * P].rearrange("p (g j) -> p g j", j=BLK),
                                                 start=(h == 0), stop=True, skip_group_check=True)
                        for g in mixed_blocks(rt, lt):
                            blk = lt * (P // BLK) + g
                            y = rt * P - blk * BLK + YOFF
                            for pq, pe_ in TPROD:
                                q = bq[:, s, pq, hq * Q4:(hq + 1) * Q4].rearrange("p h j g -> p (h j) g")[:, :, blk]
                                m = nc.tensor.matmul(ps[:, g * Q4 * BLK:(g + 1) * Q4 * BLK], toep[:, kind, pe_, y:y + P], q,
                                                     start=False, stop=True, skip_group_check=True)
                    m.then_inc(b_full, 1)

                def values(n, q, r, s):
                    hq, rt = r // LT, r % LT
                    if rt == 0:
                        pe.wait_ge(o_free, q + 1)
                    pe.wait_ge(e_done, 2 * n + 4)
                    p = prob[:, r % 2].rearrange("p (g h j) -> p g h j", h=Q4, j=BLK)
                    for h in range(Q4):
                        m = nc.tensor.matmul(ps_o[32 * h:32 * h + VW], vt[:, s, rt, hq * Q4 + h], p[:, :, h],
                                             start=(rt == 0), stop=(rt == LT - 1), tile_position=(0, 32 * h))
                    m.then_inc(p_free, 1)

                def max_rows(i, n, s):
                    pe.wait_ge(a_free, NBLK * (n + 1) + 2)
                    pe.wait_ge(m_free, i + 1)
                    nc.tensor.transpose(ps_m[0:NBLK, 0:P], mcol[:, s], ident[:]).then_inc(m_full, 1)

                def turn_sums(i, q, slot):
                    pe.wait_ge(o_free, q + 2)
                    pe.wait_ge(m_free, i + 1)
                    for lt in range(LT):
                        m = nc.tensor.transpose(ps_m[:, lt * P:(lt + 1) * P], osb[:, slot, lt * P:(lt + 1) * P], ident[:])
                    m.then_inc(m_full, 1)

                def turn_output(i):
                    pe.wait_ge(m_free, i + 1)
                    for lt in range(LT):
                        m = nc.tensor.transpose(ps_m[:, lt * P:(lt + 1) * P], onorm[:, lt].rearrange("p q h d -> p (q h d)"), ident[:])
                    m.then_inc(m_full, 1)

                def output(i, b):
                    pe.wait_ge(m_free, i + 1)
                    pe.wait_ge(r_free, INNER * b + INNER + 2)
                    for lt in range(LT):
                        ps = ps_m[:, lt * P:(lt + 1) * P]
                        c = lt % 2 * P
                        nc.tensor.matmul(ps, oT[:, lt * P:(lt + 1) * P], wo_t[:], start=(lt == 0), stop=True, skip_group_check=True)
                        m = nc.tensor.matmul(ps, gT[:, c:c + P], wout2[:, lt // 2], start=False, stop=True, skip_group_check=True)
                    m.then_inc(m_full, 1)

                def body(b, first, last):
                    for hg in range(NG):
                        n = 2 * b + hg
                        pe.wait_ge(d_b[hg], 16 * NDB * (b + 1))
                        pe.wait_ge(d_m[hg], 16 * (b + 1))
                        pe.wait_ge(g_hi, n + 1)
                        pe.wait_ge(g_lo, n + 1)
                        for u in range(NU):
                            if u == U_A and has(2, hg, last):
                                a_ready(b + 1, hg)
                            for ahead, g in a_units(hg, u):
                                if has(ahead, hg, last):
                                    a_unit(NBLK * (n + ahead) + g, g, (hg + ahead) % 2)
                            b_unit(NU * n + u, u, hg)
                            r = NP * n + u // 2
                            if u % 2 == 0 and u >= 2:
                                values(r - 1, NQ * n + (u // 2 - 1) // LT, u // 2 - 1, hg)
                            if u == 0 and not (first and hg == 0):
                                values(r - 1, NQ * n - 1, NP - 1, 1 - hg)
                            if u == 1 and not (first and hg == 0):
                                turn_sums(misc(b, T1 if hg else T3), NQ * n - 1, 1)
                            if u == 3 and hg == 0 and not first:
                                turn_output(misc(b, OT))
                            if u == 5 and hg == 0 and not first:
                                output(misc(b, OUT), b - 1)
                            if u == 9:
                                turn_sums(misc(b, T2 if hg else T0), NQ * n, 0)
                            if u == U_A and has(1, hg, last):
                                max_rows(misc(b, MAX2 if hg else MAX1), n + 1, 1 - hg)

                a_ready(0, 0)
                for g in range(NBLK):
                    a_unit(g, g, 0)
                max_rows(0, 0, 0)
                a_ready(0, 1)
                for g in range(A0):
                    a_unit(NBLK + g, g, 1)
                pe.wait_ge(s_zero, 1)
                body(0, True, False)
                with pe.Fori(1, B - 1) as b:
                    body(b, False, False)
                body(B - 1, False, True)
                values(NP * 2 * B - 1, NQ * 2 * B - 1, NP - 1, 1)
                turn_sums(misc(B - 1, NMISC + T3, True), NQ * 2 * B - 1, 1)
                turn_output(misc(B - 1, NMISC + OT, True))
                output(misc(B - 1, NMISC + OUT, True), B - 1)

            @block.vector
            def _(dve):
                def maximum(a, g, s):
                    dve.wait_ge(a_full, a + 1)
                    nc.vector.tensor_reduce(mcol[:, s, g:g + 1], ps_a[:, g % 2], AX_X, ALU.max, negate=True).then_inc(a_free, 1)

                def max_rows(i, s):
                    dve.wait_ge(m_full, i + 1)
                    nc.vector.tensor_copy(mrow[:, s], ps_m[0:NBLK, 0:P]).then_inc(m_free, 1)

                def sums(n, slot):
                    dve.wait_ge(p_free, LT * (n + 1) + 2)
                    nc.vector.tensor_copy(osb[:, slot], ps_o[:]).then_inc(o_free, 1)

                def divide(i, n, q):
                    dve.wait_ge(m_full, i + 1)
                    ps = ps_m[:].rearrange("p (t h i) -> p t h i", t=LT, h=Q4)
                    nc.vector.reciprocal(rden[:, q % 2], ps[:, :, :, D]).then_inc(s_rec, 1)
                    dve.wait_ge(s_rec, n + 1)
                    nc.vector.tensor_tensor(onorm[:, :, q], ps[:, :, :, 0:D],
                                            rden[:, q % 2].unsqueeze(3).broadcast_to([P, LT, Q4, D]), ALU.mult).then_inc(m_free, 1)

                def unit_sum(b, k):
                    n = INNER * b + k
                    dve.wait_ge(r_full, n + 2)
                    if k == 0:
                        nc.vector.tensor_scalar(acc[:, 0], relu[:, 0], t["w2c"][:, 0:1], t["b2c"][:, 0:1], ALU.mult,
                                                ALU.add).then_inc(r_free, 1)
                    else:
                        dve.wait_ge(r_free, n + 2)
                        out = gT[:] if k == INNER - 1 else acc[:, k % 2]
                        nc.vector.scalar_tensor_tensor(out=out, in0=relu[:, k % 2], scalar=t["w2c"][:, k:k + 1],
                                                       in1=acc[:, 1 - k % 2], op0=ALU.mult, op1=ALU.add).then_inc(r_free, 1)

                def copy_oT(i):
                    dve.wait_ge(m_full, i + 1)
                    nc.vector.tensor_copy(oT[:], ps_m[:]).then_inc(m_free, 1)

                def result(i, b):
                    dve.wait_ge(m_full, i + 1)
                    nc.vector.tensor_tensor(base[:, b], base[:, b], ps_m[:].rearrange("p (n f) -> p n f", n=LT),
                                            ALU.add).then_inc(m_free, 1)

                def body(b, first, last):
                    for hg in range(NG):
                        n = 2 * b + hg
                        before = not (first and hg == 0)
                        for u in range(NU):
                            if u == 1 and before:
                                sums(NQ * n - 1, 1)
                            if u == 9:
                                sums(NQ * n, 0)
                            if u == U_A + 1 and has(1, hg, last):
                                max_rows(misc(b, MAX2 if hg else MAX1), 1 - hg)
                            for ahead, g in a_units(hg, u):
                                if has(ahead, hg, last):
                                    maximum(NBLK * (n + ahead) + g, g, (hg + ahead) % 2)
                            if u == 2 and before:
                                divide(misc(b, T1 if hg else T3), NQ * n - 1, 1 if hg else 3)
                            if u == 4 and hg == 0 and not first:
                                copy_oT(misc(b, OT))
                            if u == 6 and hg == 0 and not first:
                                result(misc(b, OUT), b - 1)
                            if u == 10:
                                divide(misc(b, T2 if hg else T0), NQ * n, 2 * hg)
                            if u == 5 and has(1, hg, last):
                                if not (first and hg == 0):
                                    dve.wait_ge(b_full, NU * n)
                                dve.wait_ge(g_a, 2 * (n + 2))
                                nc.vector.tensor_copy(bq[:, 1 - hg, 0], bqa[:, 1 - hg]).then_inc(g_hi, 1)
                            if u % 2 == 1:
                                unit_sum(b, (NU * hg + u) // 2)

                dve.sem_inc(a_free, 2)
                dve.sem_inc(o_free, 1)
                dve.sem_inc(m_free, 1)
                dve.sem_inc(r_free, 2)
                nc.vector.memset(kst[32:KROWS + 1], 1.0).then_inc(s_ones, 1)
                nc.vector.memset(ps_o[:], 0.0).then_inc(s_zero, 1)
                dve.wait_ge(g_a, 2)
                nc.vector.tensor_copy(bq[:, 0, 0], bqa[:, 0]).then_inc(g_hi, 1)
                for g in range(NBLK):
                    maximum(g, g, 0)
                max_rows(0, 0)
                for g in range(A0):
                    maximum(NBLK + g, g, 1)
                body(0, True, False)
                with dve.Fori(1, B - 1) as b:
                    body(b, False, False)
                body(B - 1, False, True)
                sums(NQ * 2 * B - 1, 1)
                divide(misc(B - 1, NMISC + T3, True), NQ * 2 * B - 1, 3)
                copy_oT(misc(B - 1, NMISC + OT, True))
                result(misc(B - 1, NMISC + OUT, True), B - 1)

            @block.scalar
            def _(act):
                act.sem_inc(e_done, 2)
                act.sem_inc(p_free, 2)
                act.sem_inc(r_full, 1)

                def body(b):
                    for u in range(2 * NU):
                        n = 2 * NU * b + u
                        if u == 0:
                            act.wait_ge(r_full, INNER * b + 1)
                        act.wait_ge(b_full, n + 1)
                        if u % 2 == 0:
                            act.wait_ge(p_free, NU * b + u // 2 + 1)
                        nc.scalar.activation(prob[:, u // 2 % 2, u % 2 * 2 * L:(u % 2 + 1) * 2 * L], ps_b[:, u % 2],
                                             ACT.Exp).then_inc(e_done, 1)
                        if u % 2 == 0:
                            k = u // 2
                            if k == 0:
                                nc.scalar.copy(s_cur[:], s_all[:, b]).then_inc(s_cp, 1)
                            act.wait_ge(s_cp, b + 1)
                            act.wait_ge(r_free, INNER * b + k + 1)
                            nc.scalar.activation(relu[:, k % 2], s_cur[:], ACT.Relu, bias=t["b1c"][:, k:k + 1],
                                                 scale=t["w1c"][:, k:k + 1]).then_inc(r_full, 1)

                with act.Fori(0, B) as b:
                    body(b)


_INS = ["L0_attn_hidden_states", "L0_attn_Wq", "L0_attn_bq", "L0_attn_Wk", "L0_attn_bk", "L0_attn_Wv", "L0_attn_bv",
        "L0_attn_Wo", "L0_attn_bo", "L0_attn_dist_emb", "L0_ffn_Win", "L0_ffn_bin_", "L0_ffn_W1", "L0_ffn_b1",
        "L0_ffn_W2", "L0_ffn_b2", "L0_ffn_Wout", "L0_ffn_bout"]


def kernel(**inputs):
    import numpy as _np
    import concourse.bacc as _bacc
    from concourse import mybir as _mybir
    from concourse.bass_utils import run_bass_kernel_spmd as _run

    nc = _bacc.Bacc("TRN2", target_bir_lowering=False, num_devices=1)
    arrays, args = {}, []
    for name in _INS:
        a = _np.ascontiguousarray(inputs[name])
        arrays[f"in_{name}_dram"] = a
        args.append(nc.dram_tensor(f"in_{name}_dram", a.shape, _mybir.dt.from_np(a.dtype), kind="ExternalInput").ap())
    args.append(nc.dram_tensor("out_0_dram", (B, L, H), _mybir.dt.from_np(_np.dtype("float32")), kind="ExternalOutput").ap())
    build(nc, *args)
    r = _run(nc, [arrays], core_ids=[0])
    return r.results[0]["out_0_dram"]
```

```python
from contextlib import ExitStack

import concourse.bass as bass
from concourse import mybir

F32 = mybir.dt.float32
BF16 = mybir.dt.bfloat16
F16 = mybir.dt.float16
ALU = mybir.AluOpType
ACT = mybir.ActivationFunctionType
AX_X = mybir.AxisListType.X

B, L, H = 8, 512, 128
NH, D = 16, 8
LEFT, RIGHT = 64, 8
NPOS = LEFT + RIGHT + 1
M, INNER = 64, 16
P = 128
LT = L // P
BLK = P // D
NBLK = L // BLK
G = 8
NG = NH // G
Q4 = 4
NQ = G // Q4
LN_EPS = 1e-5
SCALE = float(D) ** -0.5
PROD = [(0, 0), (0, 1), (0, 2), (1, 0), (1, 1), (2, 0)]
KROWS = len(PROD) * D
MROW = KROWS
K_MID, K_LEFT, K_RIGHT = range(3)
LW = L - BLK - LEFT
RBEG = BLK + RIGHT
KW = LW + L + (L - RBEG)
KPOS = (LW, 0, LW + L - RBEG)
VW = 16
YOFF = P + LEFT - BLK
YLEN = YOFF + P + BLK
XOFF = YOFF + BLK - 1
XLEN = YLEN + BLK - 1
HB = BLK // 2
YOFF2, YLEN2 = YOFF + HB, YLEN + HB


def tile_kind(rt, lt):
    return K_MID if rt == lt else K_RIGHT if lt < rt else K_LEFT


def mixed_blocks(rt, lt):
    out = []
    for g in range(P // BLK):
        d0 = (lt - rt) * P + g * BLK
        right = -d0 - (BLK - 1) >= RIGHT
        left = P - 1 - d0 <= -LEFT
        if not (right or left):
            out.append(g)
    return out


def mixed_halves(rt, blk):
    out = []
    for jh in range(2):
        d0 = blk * BLK + jh * HB - rt * P
        if not (-d0 - (HB - 1) >= RIGHT or P - 1 - d0 <= -LEFT):
            out.append(jh)
    return out


def build(nc, hidden, Wq, bq, Wk, bk, Wv, bv, Wo, bo, emb, Win, bin_, W1, b1, W2, b2, Wout, bout, out):
    qk_d = nc.dram_tensor("qk_parts", [3, P, B, L + KW], BF16, kind="Internal").ap()
    qd_d = nc.dram_tensor("q_blocked", [P, B, BLK, NBLK], BF16, kind="Internal").ap()
    qc_d = nc.dram_tensor("q_half_parts", [NG, B, BLK, D, G, 2, NBLK], F16, kind="Internal").ap()
    v_d = nc.dram_tensor("v_rows", [P, B, LT, NH, VW], F32, kind="Internal").ap()
    m_d = nc.dram_tensor("max_rows", [2, G, NBLK, BLK], BF16, kind="Internal").ap()
    x_t = hidden.rearrange("b (t p) f -> p b t f", p=P)
    o_t = out.rearrange("b (t p) f -> p b t f", p=P)

    with ExitStack() as whole:
        def sb(ctx, name, shape, dt):
            return ctx.enter_context(nc.sbuf_tensor(name, shape, dt))

        base = sb(whole, "base", [P, B, LT, H], F32)
        s_all = sb(whole, "s_all", [P, B, L // 2], F32)
        ident = sb(whole, "ident", [P, P], F32)
        toep = sb(whole, "toep", [P, 3, YLEN], F16)
        toep2 = sb(whole, "toep2", [P, 3, YLEN2], F16)
        wo_t = sb(whole, "wo_t", [P, H], F32)
        wout2 = sb(whole, "wout2", [P, 2, H], F32)
        mask_f = sb(whole, "mask_f", [P, BLK], F32)
        mask_h = sb(whole, "mask_h", [P, BLK], F16)
        mask_2 = sb(whole, "mask_2", [P, HB], F16)
        w1c = sb(whole, "w1c", [P, INNER], F32)
        b1c = sb(whole, "b1c", [P, INNER], F32)
        w2c = sb(whole, "w2c", [P, INNER], F32)
        b2c = sb(whole, "b2c", [P, 1], F32)

        layer(nc, sb, locals())


def layer(nc, sb, t):
    x_t, base, s_all, ident, toep, toep2 = t["x_t"], t["base"], t["s_all"], t["ident"], t["toep"], t["toep2"]
    wo_t, wout2, mask_f, mask_h, mask_2 = t["wo_t"], t["wout2"], t["mask_f"], t["mask_h"], t["mask_2"]
    with ExitStack() as ctx:
        def pb(name, shape, dt=F32):
            return ctx.enter_context(nc.psum_tensor(name, shape, dt))

        def sem(name):
            return ctx.enter_context(nc.semaphore(name))

        qst = sb(ctx, "qst", [P, G, L], BF16)
        kst = sb(ctx, "kst", [P, G, KW], BF16)
        vt = sb(ctx, "vt", [P, 2, LT, G, VW], F32)
        qc = sb(ctx, "qc", [P, 2, G, 2, NBLK], F16)
        qc2 = sb(ctx, "qc2", [P, G, 2, NBLK], F16)
        bqa = sb(ctx, "bqa", [P, 2, G, BLK, NBLK], F16)
        bql = sb(ctx, "bql", [P, 2, G, BLK, NBLK], F16)
        bq2 = sb(ctx, "bq2", [P, 2, G, HB, 2, NBLK], F16)
        qx = sb(ctx, "qx", [P, L], BF16)
        bd = sb(ctx, "bd", [P, G, L], BF16)
        ka = sb(ctx, "ka", [P, KW], BF16)
        prob = sb(ctx, "prob", [P, 2, LT * (P // BLK) * Q4 * BLK], F32)
        osb = sb(ctx, "osb", [P, 2, L], F32)
        rden = sb(ctx, "rden", [P, 2, 2, G], F32)
        onorm = sb(ctx, "onorm", [P, LT, NG, G, D], F32)
        oT = sb(ctx, "oT", [P, L], F32)
        s_cur = sb(ctx, "s_cur", [P, L // 2], F32)
        relu = sb(ctx, "relu", [P, 2, L // 2], F32)
        acc = sb(ctx, "acc", [P, 2, L // 2], F32)
        gT = sb(ctx, "gT", [P, L // 2], F32)
        mcol = sb(ctx, "mcol", [P, 2, NBLK], F32)
        mrow = sb(ctx, "mrow", [NBLK, 2, P], BF16)
        wT = sb(ctx, "wT", [P, 3, H], F32)
        win = sb(ctx, "win", [P, M], F32)
        colb = sb(ctx, "colb", [P, 8], F32)
        colc = sb(ctx, "colc", [P, 4], F32)
        rows = sb(ctx, "rows", [P, 4, H], F32)
        xn = sb(ctx, "xn", [P, LT, H], F32)
        xT = sb(ctx, "xT", [P, L], F32)
        stats = sb(ctx, "stats", [P, B, LT, 6], F32)
        mv = sb(ctx, "mv", [P, B, LT, 2], F32)
        var = sb(ctx, "var", [P, B, LT], F32)
        std = sb(ctx, "std", [P, B, LT], F32)
        tmp = sb(ctx, "tmp", [P, 3, B, LT], F32)
        rstd = sb(ctx, "rstd", [P, B, LT], F32)
        qkf = sb(ctx, "qkf", [P, L + KW], F32)
        rem = sb(ctx, "rem", [P, L + KW], F32)
        parts = sb(ctx, "parts", [P, 3, L + KW], BF16)
        qd = sb(ctx, "qd", [P, BLK, NBLK], BF16)
        qh = sb(ctx, "qh", [P, BLK, 2, NBLK], F16)
        vrow = sb(ctx, "vrow", [P, LT, NH, VW], F32)
        wraw = prob[:, 0, 0:4 * H].rearrange("p (n f) -> p n f", n=4)
        emb_sb = prob[0:NPOS, 0, 4 * H:4 * H + D]
        ep = prob[0:D, 1, 0:3 * XLEN].rearrange("p (n x) -> p n x", n=3)
        eph = prob[0:D, 1, 2 * L:4 * L].bitcast(F16)[:, 0:6 * XLEN].rearrange("p (n a x) -> p n a x", n=3, a=2)

        ps_a = pb("ps_a", [P, 2, L])
        ps_b = pb("ps_b", [P, 2, 2 * L])
        ps_o = pb("ps_o", [P, L])
        ps_m = pb("ps_m", [P, L])
        FIRST_BANKS = ((ps_m[:], ps_a[:, 0], ps_a[:, 1], ps_o[:], ps_b[:, 1, L:2 * L]),
                       (ps_m[:], ps_b[:, 1, 0:L], ps_b[:, 1, L:2 * L], ps_o[:], ps_m[:]))

        A_BANKS = (ps_a[:, 0], ps_a[:, 1], ps_b[:, 0, 0:L], ps_b[:, 0, L:2 * L])

        d_q, d_k, d_b, d_m = ([sem(f"{n}{s}") for s in range(2)] for n in ("d_q", "d_k", "d_b", "d_m"))
        s_cp, d_md = sem("s_cp"), sem("d_md")
        s_qz = sem("s_qz")
        s_ones, s_zero = [sem("s_ones0"), sem("s_ones1")], sem("s_zero")
        d_2 = sem("d_2")
        g_a, g_bd, g_b = sem("g_a"), sem("g_bd"), sem("g_b")
        g_first = sem("g_first")
        a_full, a_free = sem("a_full"), sem("a_free")
        b_full, e_done = sem("b_full"), sem("e_done")
        p_free = sem("p_free")
        o_free = sem("o_free")
        m_full, m_free = sem("m_full"), sem("m_free")
        s_rec = sem("s_rec")
        r_full, r_free = sem("r_full"), sem("r_free")
        s_done = sem("s_done")

        c_x = [sem("c_x0"), sem("c_x1")]
        c_w, c_cst, c_row, c_pad = sem("c_w"), sem("c_cst"), sem("c_row"), sem("c_pad")
        c_toep, c_toep2 = sem("c_toep"), sem("c_toep2")
        c_zero, c_ident = sem("c_zero"), sem("c_ident")
        c_wT, c_wTc = sem("c_wT"), sem("c_wTc")
        c_ebT, c_ep = sem("c_ebT"), sem("c_ep")
        c_col, c_vec, c_stats, c_var = sem("c_col"), sem("c_vec"), sem("c_stats"), sem("c_var")
        c_ln = sem("c_ln")
        t_full, q_full, k_full, v_full, s_full = (sem(n) for n in ("t_full", "q_full", "k_full", "v_full", "s_full"))
        t_free, q_free, k_free, v_free, s_free = (sem(n) for n in ("t_free", "q_free", "k_free", "v_free", "s_free"))
        c_hi, c_hb, c_rem, c_mid, c_lo = (sem(n) for n in ("c_hi", "c_hb", "c_rem", "c_mid", "c_lo"))
        c_ql, c_base, c_outq, c_out = sem("c_ql"), sem("c_base"), sem("c_outq"), sem("c_out")
        NW, NCST, NROW, NPAD = 5, 5, 5, 8 + 2
        NREM = 3
        KH = KW // 2
        NSQ, NST = 16 * (1 + NH), 16 * 3

        NDQ = 2
        NDB = 2 * len(PROD) + 1
        NU = LT * LT
        A0 = 10
        NPAIR = LT // 2
        T3, OT, OUT, MAX1, T0, T1, T2, MAX2 = range(8)
        NMISC = 8

        def slot(s):
            return slice(64 * s, 64 * s + 64)

        def misc(b, i, last=False):
            return NMISC * b + i - 2 - (1 if last and i >= NMISC else 0)

        GB = P // BLK // 2

        def unit(u):
            return u // 2 % LT, u // (2 * LT) * 2 + u % 2

        def spacing():
            other = {0: {3: 1024, 5: 1024, 7: 2048, 8: 1024, 10: 2048, 13: 1024},
                     1: {3: 1024, 5: 2048, 7: 1024, 11: 1024}}
            plan = []
            for hg in range(NG):
                work = []
                for u in range(NU):
                    rt, lt = unit(u)
                    tiles = [L + 2 * G * BLK * len([g for g in mixed_blocks(rt, lt) if g // GB == i]) for i in range(2)]
                    work += [0, tiles[0], tiles[1]]
                    if u < NU - 1:
                        work.append(2 * L + other[hg].get(u, 0))
                total, done, k = sum(work), 0, 0
                places = []
                i = 0
                for u in range(NU):
                    places.append([])
                    for place in range(3):
                        done += work[i]
                        i += 1
                        here = []
                        while k < NBLK and done * NBLK >= (k + 0.3) * total:
                            here.append((1, A0 + k) if k < NBLK - A0 else (2, k - (NBLK - A0)))
                            k += 1
                        places[-1].append(here)
                    if u < NU - 1:
                        done += work[i]
                        i += 1
                while k < NBLK:
                    places[-1][-1].append((2, k - (NBLK - A0)))
                    k += 1
                plan.append(places)
            return plan

        PLAN = spacing()
        U_LAST = [max(u for u in range(NU) if any((1, NBLK - 1) in place for place in PLAN[hg][u])) for hg in range(NG)]

        assert U_LAST == [11, 11], U_LAST

        def has(n_ahead, hg, last):
            return not last or hg + n_ahead < NG

        def batches(eng, body):
            body(0, True, False, True)
            with eng.Fori(1, B - 2) as b:
                body(b, False, False, True)
            body(B - 2, False, False, False)
            body(B - 1, False, True, False)

        with nc.Block() as block:
            @block.sync
            def _(sp):
                def load_q(b, hg):
                    sp.dma_start(qc[:, hg].rearrange("p h a g -> p (h a g)"),
                                 t["qc_d"][hg, b].rearrange("j d h a g -> (j d) (h a g)")).then_inc(d_q[hg], 16)
                    sp.dma_start(qx[slot(hg)], t["qd_d"][hg * G * D:(hg + 1) * G * D, b].rearrange("p j g -> p (j g)")).then_inc(d_q[hg], 16)

                def load_2(b, hg):
                    for twice in range(2):
                        for jh in range(2):
                            sp.dma_start(qc2[slot(twice), :, jh],
                                         t["qc_d"][hg, b, jh * HB:(jh + 1) * HB, :, :, 0].rearrange("j d h g -> (j d) h g")).then_inc(d_2, 16)

                def load_k(b, hg):
                    sp.dma_start(ka[slot(hg)], t["qk_d"][0, hg * G * D:(hg + 1) * G * D, b, L:]).then_inc(d_k[hg], 16)

                def load_b(b, hg):
                    hd = slice(hg * G * D, (hg + 1) * G * D)
                    for n, (pq, pk) in enumerate(PROD):
                        r = slice(64 * hg + n * D, 64 * hg + (n + 1) * D)
                        for dst, src in ((qst[r], t["qk_d"][pq, hd, b, 0:L]), (kst[r], t["qk_d"][pk, hd, b, L:])):
                            sp.dma_start(dst, src.rearrange("(h d) l -> d h l", h=G)).then_inc(d_b[hg], 16)

                def load_v(b, hg):
                    sp.dma_start(vt[:, hg], t["v_d"][:, b, :, hg * G:(hg + 1) * G]).then_inc(d_b[hg], 16)

                def max_row(n, s, i):
                    sp.wait_ge(m_free, i + 2)
                    sp.dma_start(t["m_d"][s].rearrange("h g j -> g h j"), mrow[:, s].rearrange("g (h j) -> g h j", h=G)).then_inc(d_md, 16)
                    sp.wait_ge(d_md, 16 * (n + 1))
                    r = 64 * s + MROW
                    sp.dma_start(qst[r:r + 1], t["m_d"][s].rearrange("h g j -> (h g j)").rearrange("(a h l) -> a h l", a=1, h=G)).then_inc(d_m[s], 16)

                def store(b, i):
                    sp.wait_ge(m_free, i + 2)
                    sp.dma_start(t["o_t"][:, b], base[:, b]).then_inc(s_done, 16)

                def store_q(p):
                    sp.wait_ge(c_ql, p + 1)
                    sp.dma_start(t["qd_d"][:, p], qd[:]).then_inc(c_outq, 16)
                    for h in range(NH):
                        sp.dma_start(t["qc_d"][h // G, p, :, :, h % G].rearrange("j d a g -> d j (a g)"),
                                     qh[h * D:(h + 1) * D].rearrange("d j a g -> d j (a g)")).then_inc(c_outq, 16)

                def store_v(p):
                    sp.wait_ge(v_free, p + 1)
                    sp.dma_start(t["v_d"][:, p], vrow[:]).then_inc(c_out, 16)

                def store_first(p):
                    sp.wait_ge(c_hi, 2 * p + 2)
                    sp.dma_start(t["qk_d"][0, :, p], parts[:, 0]).then_inc(c_out, 16)

                def store_rest(p):
                    sp.wait_ge(c_lo, NREM * p + NREM)
                    sp.dma_start(t["qk_d"][1:3, :, p].rearrange("a p l -> p a l"), parts[:, 1:3]).then_inc(c_out, 16)

                def body(b, first, last, prep):
                    const = first or last or not prep
                    nxt = b + 1 if const else sp.snap(b + 1)
                    for hg in range(NG):
                        n = 2 * b + hg
                        if has(1, hg, last):
                            if first and hg == 0:
                                sp.wait_ge(b_full, 1)
                            else:
                                sp.wait_ge(p_free, NU * n + 3)
                            load_v(nxt if hg else b, 1 - hg)
                        if has(2, hg, last):
                            if hg == 0:
                                sp.wait_ge(c_outq, NSQ * (b + 2))
                            load_q(nxt, hg)
                        if has(1, hg, last):
                            load_2(nxt if hg else b, 1 - hg)
                        if first and hg == 0:
                            store_rest(1)
                        if has(2, hg, last):
                            if hg == 0:
                                sp.wait_ge(c_out, NST * (b + 2))
                            load_k(nxt, hg)
                        if has(1, hg, last):
                            load_b(nxt if hg else b, 1 - hg)
                        if hg == 0 and not first:
                            store(b - 1, misc(b, OUT))
                        if hg == 1 and prep:
                            store_q(b + 2)
                        if has(1, hg, last):
                            max_row(n + 1, 1 - hg, misc(b, MAX1 if hg == 0 else MAX2))
                        if hg == 1 and prep:
                            store_v(b + 2)
                            store_first(b + 2)
                            store_rest(b + 2)

                def on_rows(v, n):
                    return bass.AP(v.tensor, v.offset, [[0, n], [1, H]])

                for b in range(2):
                    sp.dma_start(base[:, b], x_t[:, b]).then_inc(c_x[0], 16)
                for n, w in enumerate(("Wq", "Wk", "Wv", "Wo")):
                    sp.dma_start(wraw[:, n], t[w]).then_inc(c_w, 16)
                sp.dma_start(emb_sb, t["emb"]).then_inc(c_w, 16)
                sp.dma_start(win[:], t["Win"]).then_inc(c_cst, 16)
                sp.dma_start(colb[:, 0:1], t["bq"].rearrange("(p a) -> p a", a=1)).then_inc(c_cst, 16)
                sp.dma_start(colb[:, 1:2], t["bk"].rearrange("(p a) -> p a", a=1)).then_inc(c_cst, 16)
                for n, row in ((2, 0), (3, NPOS - 1)):
                    e = t["emb"][row]
                    sp.dma_start(colb[:, n:n + 1], bass.AP(e.tensor, e.offset, [[0, NH], [1, D], [1, 1]])).then_inc(c_cst, 16)
                for n, v in enumerate(("bv", "bo", "bout")):
                    sp.dma_start(rows[:, n], on_rows(t[v], P)).then_inc(c_row, 16)
                for h in range(2):
                    half = slice(M * h, M * h + M)
                    sp.dma_start(colb[half, 4:5], t["bin_"].rearrange("(p a) -> p a", a=1)).then_inc(c_row, 16)
                sp.dma_start(base[:, 2:B], x_t[:, 2:B]).then_inc(c_x[1], 16)
                for h in range(2):
                    half = slice(M * h, M * h + M)
                    sp.dma_start(t["b2c"][half], t["b2"].rearrange("(p a) -> p a", a=1)).then_inc(c_pad, 16)
                    sp.dma_start(t["w1c"][half], t["W1"]).then_inc(c_pad, 16)
                    sp.dma_start(t["b1c"][half], t["b1"]).then_inc(c_pad, 16)
                    sp.dma_start(t["w2c"][half], t["W2"]).then_inc(c_pad, 16)
                sp.wait_ge(c_zero, 3)
                for h in range(2):
                    sp.dma_start(wout2[M * h:M * h + M, h], t["Wout"]).then_inc(c_pad, 16)
                store_q(0)
                store_first(0)
                sp.wait_ge(c_outq, NSQ)
                load_q(0, 0)
                sp.wait_ge(c_out, 16)
                load_k(0, 0)
                load_2(0, 0)
                load_q(0, 1)
                load_k(0, 1)
                store_v(0)
                store_rest(0)
                for part in range(2):
                    for j in range(HB):
                        r = 64 * part + j * D
                        sp.dma_start(toep2[r:r + D], eph[:, :, part, HB - 1 - j:HB - 1 - j + YLEN2]).then_inc(c_toep2, 16)
                sp.wait_ge(c_out, NST)
                sp.wait_ge(s_ones[0], 1)
                sp.wait_ge(s_qz, 1)
                load_v(0, 0)
                load_b(0, 0)
                store_first(1)
                max_row(0, 0, 0)
                store_q(1)
                store_v(1)
                sp.wait_ge(s_ones[1], 2)
                batches(sp, body)
                store(B - 1, misc(B - 1, NMISC + OUT, True))
                sp.wait_ge(s_done, 16 * B)

            @block.gpsimd
            def _(pool):
                def spread(out, s, part):
                    return nc.gpsimd.tensor_tensor(out, qc[:, s, :, part].unsqueeze(2).broadcast_to([P, G, BLK, NBLK]),
                                                   mask_h[:].unsqueeze(1).unsqueeze(3).broadcast_to([P, G, BLK, NBLK]), ALU.mult)

                def spread_2(s):
                    q2 = qc2[:].rearrange("p h x g -> p h (x g)").unsqueeze(2).broadcast_to([P, G, HB, 2 * NBLK])
                    return nc.gpsimd.tensor_tensor(bq2[:, s].rearrange("p h j x g -> p h j (x g)"), q2,
                                                   mask_2[:].unsqueeze(1).unsqueeze(3).broadcast_to([P, G, HB, 2 * NBLK]), ALU.mult)

                def biases(p):
                    pool.wait_ge(c_ln, p + 1)
                    nc.gpsimd.tensor_tensor(base[:, p], base[:, p], rows[:, 3:4].broadcast_to([P, LT, H]), ALU.add).then_inc(c_base, 1)

                def lowest(p):
                    for i, c in enumerate((slice(0, L), slice(L, L + KH), slice(L + KH, L + KW))):
                        pool.wait_ge(c_mid, NREM * p + i + 1)
                        nc.gpsimd.tensor_tensor(parts[:, 2, c], rem[:, c], parts[:, 1, c], ALU.subtract).then_inc(c_lo, 1)

                def body(b, first, last, prep):
                    for hg in range(NG):
                        n = 2 * b + hg
                        if has(2, hg, last):
                            pool.wait_ge(d_q[hg], 16 * NDQ * (b + 2))
                            spread(bqa[:, hg], hg, 0).then_inc(g_a, 1)
                        if has(1, hg, last):
                            pool.wait_ge(d_2, 16 * 4 * (n + 2))
                            spread_2(1 - hg).then_inc(g_b, 1)
                            spread(bql[:, 1 - hg], 1 - hg, 1).then_inc(g_b, 1)
                        if prep and hg == 0:
                            biases(b + 2)
                        if prep and hg == 1:
                            lowest(b + 2)

                nc.gpsimd.memset(ident[:], 0.0).then_inc(c_zero, 1)
                nc.gpsimd.memset(mask_f[:], 1.0).then_inc(c_zero, 1)
                nc.gpsimd.memset(wout2[:], 0.0).then_inc(c_zero, 1)
                pool.wait_ge(c_zero, 3)
                nc.gpsimd.affine_select(out=ident[:], in_=ident[:], compare_op=ALU.not_equal, fill=1.0, base=0,
                                        pattern=[[-1, P]], channel_multiplier=1).then_inc(c_ident, 1)
                nc.gpsimd.affine_select(out=mask_f[:], in_=mask_f[:], compare_op=ALU.is_ge, fill=0.0, base=0,
                                        pattern=[[-D, BLK]], channel_multiplier=1).then_inc(c_ident, 1)
                pool.wait_ge(c_ident, 2)
                nc.gpsimd.affine_select(out=mask_f[:], in_=mask_f[:], compare_op=ALU.is_ge, fill=0.0, base=D - 1,
                                        pattern=[[D, BLK]], channel_multiplier=-1).then_inc(c_ident, 1)
                pool.wait_ge(c_ident, 3)
                nc.gpsimd.tensor_copy(mask_h[:], mask_f[:]).then_inc(c_ident, 1)
                for s in range(2):
                    pool.wait_ge(c_ident, 4 + s)
                    nc.gpsimd.tensor_copy(mask_2[slot(s)], mask_f[slot(s), HB * s:HB * s + HB]).then_inc(c_ident, 1)
                pool.wait_ge(c_ident, 6)
                nc.gpsimd.memset(kst[32:64], 1.0).then_inc(s_ones[0], 1)
                pool.wait_ge(s_ones[0], 1)
                pool.wait_ge(c_ep, 3)
                for j in range(BLK):
                    pool.dma_start(toep[j * D:(j + 1) * D], eph[:, :, 0, BLK - 1 - j:BLK - 1 - j + YLEN]).then_inc(c_toep, 16)
                lowest(0)
                pool.wait_ge(d_2, 16 * 4)
                spread_2(0).then_inc(g_b, 1)
                pool.wait_ge(d_q[1], 16 * NDQ)
                spread(bqa[:, 1], 1, 0).then_inc(g_a, 1)
                pool.wait_ge(d_q[0], 16 * NDQ)
                spread(bql[:, 0], 0, 1).then_inc(g_b, 1)
                pool.wait_ge(c_row, 16 * NROW + 1)
                lowest(1)
                biases(0)
                biases(1)
                batches(pool, body)

            @block.tensor
            def _(pe):
                def turn_x(p, ps):
                    pe.wait_ge(c_ln, p + 1)
                    for n in range(LT):
                        m = nc.tensor.transpose(ps[:, n * P:(n + 1) * P], xn[:, n], ident[:])
                    m.then_inc(t_full, 1)

                def project_q(p, ps):
                    pe.wait_ge(t_free, p + 1)
                    nc.tensor.matmul(ps, wT[:, 0], xT[:], start=True, stop=True).then_inc(q_full, 1)

                def project_k(p, ps):
                    nc.tensor.matmul(ps, wT[:, 1], xT[:], start=True, stop=True).then_inc(k_full, 1)

                def project_v(p, ps):
                    for n in range(LT):
                        m = nc.tensor.matmul(ps[:, n * P:(n + 1) * P], xT[:, n * P:(n + 1) * P], wT[:, 2],
                                             start=(n == 0), stop=True, skip_group_check=True)
                    m.then_inc(v_full, 1)

                def project_s(p, ps):
                    for h in range(2):
                        m = nc.tensor.matmul(ps[M * h:M * h + M, 0:L // 2], win[:], xT[:, h * (L // 2):(h + 1) * (L // 2)],
                                             start=True, stop=True)
                    m.then_inc(s_full, 1)

                def a_ready(b, hg):
                    pe.wait_ge(g_a, 2 * b + hg)
                    pe.wait_ge(g_bd, 2 * b + hg + 1)
                    pe.wait_ge(d_k[hg], 16 * (b + 1))

                def a_unit(a, g, s, banks=None):
                    ps = banks[g % len(banks)] if banks else ps_a[:, g % 2]
                    c0, c1 = max(0, g * BLK - LEFT), min(L, g * BLK + BLK + RIGHT)
                    if banks is None:
                        pe.wait_ge(a_free, a + 1)
                    elif a >= len(banks):
                        pe.wait_ge(a_free, a - len(banks) + 3)
                    first = True
                    for kind, lo, hi in ((K_LEFT, 0, c0), (K_MID, c0, c1), (K_RIGHT, c1, L)):
                        if hi > lo:
                            o = KPOS[kind]
                            nc.tensor.matmul(ps[:, lo:hi], bd[slot(s)].rearrange("p h (j g) -> p (h j) g", j=BLK)[:, :, g],
                                             ka[slot(s), o + lo:o + hi], start=first, stop=True, skip_group_check=True)
                            first = False
                    y = c0 - g * BLK + YOFF
                    nc.tensor.matmul(ps[:, c0:c1], bqa[:, s].rearrange("p h j g -> p (h j) g")[:, :, g],
                                     toep[:, K_MID, y:y + c1 - c0], start=False, stop=True, skip_group_check=True).then_inc(a_full, 1)

                def b_bank(n, u, s, x):
                    rt, lt = unit(u)
                    kind = tile_kind(rt, lt)
                    k0 = KPOS[kind] + rt * P
                    l0 = lt * P + x * (P // 2)
                    if x == 0:
                        pe.wait_ge(e_done, n + 1)
                    ps = ps_b[:, u % 2, x * L:(x + 1) * L].rearrange("p (g h j) -> p g h j", g=GB, h=G)
                    for h in range(G):
                        m = nc.tensor.matmul(ps[:, :, h], kst[slot(s), h, k0:k0 + P],
                                             qst[slot(s), h, l0:l0 + P // 2].rearrange("p (g j) -> p g j", j=BLK),
                                             start=(h == 0), stop=True, skip_group_check=True)
                    for g in range(GB):
                        if x * GB + g not in mixed_blocks(rt, lt):
                            continue
                        blk = lt * (P // BLK) + x * GB + g
                        for jh in mixed_halves(rt, blk):
                            y = rt * P - blk * BLK - jh * HB + YOFF2
                            nc.tensor.matmul(ps[:, g, :, jh * HB:(jh + 1) * HB], toep2[:, kind, y:y + P], bq2[:, s, :, :, jh, blk],
                                             start=False, stop=True, skip_group_check=True)
                        y = rt * P - blk * BLK + YOFF
                        m = nc.tensor.matmul(ps[:, g].rearrange("p h j -> p (h j)"), toep[:, kind, y:y + P],
                                             bql[:, s].rearrange("p h j g -> p (h j) g")[:, :, blk],
                                             start=False, stop=True, skip_group_check=True)
                    if x == 1:
                        m.then_inc(b_full, 1)

                def values(n, pairs, r, q, s):
                    rt = r % LT
                    if rt == 0 and q == 0:
                        pe.wait_ge(o_free, pairs + 1)
                    if q == 0:
                        pe.wait_ge(e_done, n + 4)
                    p = prob[:, r % 2].rearrange("p (g h j) -> p g h j", h=G, j=BLK)
                    for h in range(Q4):
                        m = nc.tensor.matmul(ps_o[32 * h:32 * h + VW, q * 2 * P:(q + 1) * 2 * P], vt[:, s, rt, q * Q4 + h],
                                             p[:, :, q * Q4 + h], start=(rt == 0 and q == 0), stop=(rt == LT - 1),
                                             skip_group_check=True, tile_position=(0, 32 * h))
                    m.then_inc(p_free, 1)

                def max_rows(i, n, s):
                    pe.wait_ge(a_free, NBLK * (n + 1) + 2)
                    pe.wait_ge(m_free, i + 1)
                    nc.tensor.transpose(ps_m[0:NBLK, 0:P], mcol[:, s], ident[:]).then_inc(m_full, 1)

                def turn_sums(i, q, s):
                    pe.wait_ge(o_free, q + 2)
                    pe.wait_ge(m_free, i + 1)
                    for i in range(2):
                        for j in range(NQ):
                            o = (NQ * i + j) * P
                            m = nc.tensor.transpose(ps_m[:, o:o + P], osb[:, s, (2 * j + i) * P:(2 * j + i + 1) * P], ident[:])
                    m.then_inc(m_full, 1)

                def turn_output(i):
                    pe.wait_ge(m_free, i + 1)
                    for lt in range(LT):
                        m = nc.tensor.transpose(ps_m[:, lt * P:(lt + 1) * P], onorm[:, lt].rearrange("p a h d -> p (a h d)"), ident[:])
                    m.then_inc(m_full, 1)

                def output(i, b):
                    pe.wait_ge(m_free, i + 1)
                    pe.wait_ge(r_free, INNER * b + INNER + 2)
                    for lt in range(LT):
                        ps = ps_m[:, lt * P:(lt + 1) * P]
                        c = lt % 2 * P
                        nc.tensor.matmul(ps, oT[:, lt * P:(lt + 1) * P], wo_t[:], start=(lt == 0), stop=True, skip_group_check=True)
                        m = nc.tensor.matmul(ps, gT[:, c:c + P], wout2[:, lt // 2], start=False, stop=True, skip_group_check=True)
                    m.then_inc(m_full, 1)

                def body(b, first, last, prep):
                    for hg in range(NG):
                        n = 2 * b + hg
                        pe.wait_ge(d_b[hg], 16 * NDB * (b + 1))
                        pe.wait_ge(d_m[hg], 16 * (b + 1))
                        pe.wait_ge(g_b, 2 * n + 2)
                        for u in range(NU):
                            for place in range(3):
                                for ahead, g in PLAN[hg][u][place]:
                                    if has(ahead, hg, last):
                                        if (ahead, g) == (2, 0):
                                            a_ready(b + 1, hg)
                                        a_unit(NBLK * (n + ahead) + g, g, (hg + ahead) % 2)
                                if place < 2:
                                    b_bank(NU * n + u, u, hg, place)
                            if u >= 2:
                                values(NU * n + u - 2, NPAIR * n + (u - 2) // (2 * LT), u // 2 - 1, u % 2, hg)
                            elif not (first and hg == 0):
                                values(NU * n + u - 2, NPAIR * n - 1, NU // 2 - 1, u % 2, 1 - hg)
                            if u == 3 and hg == 0 and not first:
                                turn_sums(misc(b, T3), NPAIR * n - 1, 1)
                            if u == 5 and hg == 0 and not first:
                                turn_output(misc(b, OT))
                            if u == 7 and hg == 0 and not first:
                                output(misc(b, OUT), b - 1)
                            if u == 8 and hg == 0 and prep:
                                pe.wait_ge(m_free, misc(b, OUT) + 2)
                                turn_x(b + 2, ps_m[:])
                            if u == 10 and hg == 0 and prep:
                                project_q(b + 2, ps_m[:])
                            if u == 12 and has(1, hg, last):
                                if prep:
                                    pe.wait_ge(s_free if hg else q_free, b + 3)
                                max_rows(misc(b, MAX2 if hg else MAX1), n + 1, 1 - hg)
                            if u == 13 and hg == 0:
                                turn_sums(misc(b, T0), NPAIR * n, 0)
                            if u == 15 and hg == 0 and prep:
                                pe.wait_ge(m_free, misc(b, T0) + 2)
                                project_k(b + 2, ps_m[:])
                            if u == 3 and hg == 1:
                                if prep:
                                    pe.wait_ge(k_free, b + 3)
                                turn_sums(misc(b, T1), NPAIR * n - 1, 1)
                            if u == 5 and hg == 1 and prep:
                                pe.wait_ge(m_free, misc(b, T1) + 2)
                                project_v(b + 2, ps_m[:])
                            if u == 7 and hg == 1 and prep:
                                pe.wait_ge(v_free, b + 3)
                                project_s(b + 2, ps_m[:])
                            if u == 11 and hg == 1:
                                if prep:
                                    pe.wait_ge(s_free, b + 3)
                                turn_sums(misc(b, T2), NPAIR * n, 0)

                pe.wait_ge(c_w, 16 * NW)
                pe.wait_ge(c_ident, 1)
                for n in range(4):
                    w = nc.tensor.transpose(ps_b[:, 0, n * H:(n + 1) * H], wraw[:, n], ident[:])
                w.then_inc(c_wT, 1)
                nc.tensor.transpose(ps_b[0:D, 1, 0:NPOS], emb_sb, ident[0:NPOS, 0:NPOS]).then_inc(c_ebT, 1)
                pe.wait_ge(c_wTc, 1)
                pe.wait_ge(c_cst, 16 * NCST)
                for p in range(2):
                    for project, free, ps in zip((turn_x, project_q, project_k, project_v, project_s),
                                                 ((t_free, 1), (c_ep, 1), (s_free, 1), (v_free, 1), (t_free, 2)), FIRST_BANKS[p]):
                        if p:
                            pe.wait_ge(*free)
                        project(p, ps)
                pe.wait_ge(c_toep, 16 * BLK)
                pe.wait_ge(g_first, 1)
                pe.wait_ge(q_free, 1)
                pe.wait_ge(k_free, 1)
                pe.wait_ge(g_bd, 1)
                pe.wait_ge(d_k[0], 16)
                pe.wait_ge(c_wTc, 2)
                for g in range(NBLK):
                    a_unit(g, g, 0, A_BANKS)
                pe.wait_ge(s_free, 2)
                max_rows(0, 0, 0)
                a_ready(0, 1)
                for g in range(A0):
                    a_unit(NBLK + g, g, 1)
                pe.wait_ge(q_free, 2)
                pe.wait_ge(k_free, 2)
                pe.wait_ge(s_zero, 1)
                pe.wait_ge(c_toep2, 16 * 2 * HB)
                pe.wait_ge(c_pad, 16 * NPAD)
                batches(pe, body)
                for q in range(NQ):
                    values(NU * 2 * B - 2 + q, NPAIR * 2 * B - 1, NU // 2 - 1, q, 1)
                turn_sums(misc(B - 1, NMISC + T3, True), NPAIR * 2 * B - 1, 1)
                turn_output(misc(B - 1, NMISC + OT, True))
                output(misc(B - 1, NMISC + OUT, True), B - 1)

            @block.vector
            def _(dve):
                cnt = [0]

                def link(ins):
                    cnt[0] += 1
                    ins.then_inc(c_vec, 1)
                    dve.wait_ge(c_vec, cnt[0])

                def statistics(b0, b1):
                    for b in range(b0, b1):
                        for n in range(LT):
                            m = nc.vector.bn_stats(stats[:, b, n], base[:, b, n])
                    m.then_inc(c_stats, 1)

                def inverse(b0, b1, i):
                    dve.wait_ge(c_stats, i + 1)
                    for b in range(b0, b1):
                        for n in range(LT):
                            m = nc.vector.bn_aggr(mv[:, b, n], stats[:, b, n])
                    link(m)
                    bs = slice(b0, b1)
                    nc.vector.tensor_scalar(var[:, bs], mv[:, bs, :, 1], LN_EPS, None, ALU.add).then_inc(c_var, 1)
                    dve.wait_ge(c_var, 2 * i + 2)
                    link(nc.vector.reciprocal(tmp[:, 0, bs], std[:, bs]))
                    link(nc.vector.tensor_tensor(tmp[:, 1, bs], tmp[:, 0, bs], tmp[:, 0, bs], ALU.mult))
                    link(nc.vector.tensor_tensor(tmp[:, 2, bs], tmp[:, 1, bs], var[:, bs], ALU.mult))
                    link(nc.vector.tensor_scalar(tmp[:, 1, bs], tmp[:, 2, bs], -0.5, 1.5, ALU.mult, ALU.add))
                    link(nc.vector.tensor_tensor(rstd[:, bs], tmp[:, 0, bs], tmp[:, 1, bs], ALU.mult))

                def normal(p, n0):
                    for n in range(n0, n0 + 2):
                        m = nc.vector.tensor_scalar(xn[:, n], base[:, p, n], mv[:, p, n, 0:1], rstd[:, p, n:n + 1],
                                                    ALU.subtract, ALU.mult)
                    if n0:
                        m.then_inc(c_ln, 1)

                def copy_xT(p, ps):
                    dve.wait_ge(t_full, p + 1)
                    nc.vector.tensor_copy(xT[:], ps).then_inc(t_free, 1)

                def remainder(p, i):
                    c = (slice(0, L), slice(L, L + KH), slice(L + KH, L + KW))[i]
                    dve.wait_ge(c_hi, 2 * p + (2 if i else 1))
                    nc.vector.tensor_tensor(rem[:, c], qkf[:, c], parts[:, 0, c], ALU.subtract).then_inc(c_rem, 1)

                def second_half_part(p):
                    dve.wait_ge(c_hb, 2 * p + 2)
                    nc.vector.tensor_tensor(qh[:, :, 1].rearrange("p j g -> p g j"),
                                            qkf[:, 0:L].rearrange("p (g j) -> p g j", j=BLK),
                                            qh[:, :, 0].rearrange("p j g -> p g j"), ALU.subtract).then_inc(c_ql, 1)

                def mlp_inputs(p, ps):
                    dve.wait_ge(s_full, p + 1)
                    nc.vector.tensor_scalar(s_all[:, p], ps[:, 0:L // 2], colb[:, 4:5], None, ALU.add).then_inc(s_free, 1)

                def v_rows(p, ps, stored):
                    dve.wait_ge(v_full, p + 1)
                    if stored:
                        dve.wait_ge(c_out, NST * p)
                    nc.vector.tensor_tensor(vrow[:, :, :, 0:D], ps.rearrange("p (n h d) -> p n h d", n=LT, h=NH),
                                            rows[:, 0:1].broadcast_to([P, LT, H]).rearrange("p n (h d) -> p n h d", h=NH),
                                            ALU.add).then_inc(v_free, 1)

                def maximum(a, g, s, banks=None):
                    dve.wait_ge(a_full, a + 1)
                    ps = banks[g % len(banks)] if banks else ps_a[:, g % 2]
                    nc.vector.tensor_reduce(mcol[:, s, g:g + 1], ps, AX_X, ALU.max, negate=True).then_inc(a_free, 1)

                def maxima(n, hg, u, place, last):
                    for ahead, g in PLAN[hg][u][place]:
                        if has(ahead, hg, last):
                            maximum(NBLK * (n + ahead) + g, g, (hg + ahead) % 2)

                def max_rows(i, s):
                    dve.wait_ge(m_full, i + 1)
                    nc.vector.tensor_copy(mrow[:, s], ps_m[0:NBLK, 0:P]).then_inc(m_free, 1)

                def sums(n, s):
                    dve.wait_ge(p_free, NQ * LT * (n + 1) + 3)
                    nc.vector.tensor_copy(osb[:, s], ps_o[:]).then_inc(o_free, 1)

                def divide(i, n, pair, hg):
                    dve.wait_ge(m_full, i + 1)
                    ps = ps_m[:].rearrange("p (t h i) -> p t h i", t=2, h=G)
                    nc.vector.reciprocal(rden[:, pair], ps[:, :, :, D]).then_inc(s_rec, 1)
                    dve.wait_ge(s_rec, n + 1)
                    nc.vector.tensor_tensor(onorm[:, 2 * pair:2 * pair + 2, hg], ps[:, :, :, 0:D],
                                            rden[:, pair].unsqueeze(3).broadcast_to([P, 2, G, D]), ALU.mult).then_inc(m_free, 1)

                def inputs(b):
                    dve.wait_ge(r_full, INNER * b + 1)
                    nc.vector.tensor_copy(s_cur[:], s_all[:, b]).then_inc(s_cp, 1)

                def unit_sum(b, k):
                    n = INNER * b + k
                    dve.wait_ge(r_full, n + 2)
                    if k == 0:
                        nc.vector.tensor_scalar(acc[:, 0], relu[:, 0], t["w2c"][:, 0:1], t["b2c"][:, 0:1], ALU.mult,
                                                ALU.add).then_inc(r_free, 1)
                    else:
                        dve.wait_ge(r_free, n + 2)
                        out = gT[:] if k == INNER - 1 else acc[:, k % 2]
                        nc.vector.scalar_tensor_tensor(out=out, in0=relu[:, k % 2], scalar=t["w2c"][:, k:k + 1],
                                                       in1=acc[:, 1 - k % 2], op0=ALU.mult, op1=ALU.add).then_inc(r_free, 1)

                def copy_oT(i):
                    dve.wait_ge(m_full, i + 1)
                    nc.vector.tensor_copy(oT[:], ps_m[:]).then_inc(m_free, 1)

                def result(i, b):
                    dve.wait_ge(m_full, i + 1)
                    nc.vector.tensor_tensor(base[:, b], base[:, b], ps_m[:].rearrange("p (n f) -> p n f", n=LT),
                                            ALU.add).then_inc(m_free, 1)

                def body(b, first, last, prep):
                    for hg in range(NG):
                        n = 2 * b + hg
                        before = not (first and hg == 0)
                        for u in range(NU):
                            if u == 1 and hg == 0:
                                inputs(b)
                            if u == 2 and before:
                                sums(NPAIR * n - 1, 1)
                            if u == 10:
                                sums(NPAIR * n, 0)
                            maxima(n, hg, u, 0, last)
                            if u == 4 and before:
                                divide(misc(b, T1 if hg else T3), NPAIR * n - 1, 1, 1 - hg)
                            if u == 6 and hg == 0 and not first:
                                copy_oT(misc(b, OT))
                            if u == 8 and hg == 0 and not first:
                                result(misc(b, OUT), b - 1)
                            if u == 9 and hg == 0 and prep:
                                copy_xT(b + 2, ps_m[:])
                            if u == 6 and hg == 1 and prep:
                                v_rows(b + 2, ps_m[:], True)
                            if u == (12 if hg else 14):
                                divide(misc(b, T2 if hg else T0), NPAIR * n, 0, hg)
                            if u == U_LAST[hg] + 2 and has(1, hg, last):
                                max_rows(misc(b, MAX2 if hg else MAX1), 1 - hg)
                            if u == 8 and hg == 1 and prep:
                                mlp_inputs(b + 2, ps_m[:])
                            maxima(n, hg, u, 1, last)
                            if first and hg == 0 and u < NREM:
                                remainder(1, u)
                            if prep and hg == 0 and u in (3, 4):
                                normal(b + 2, 2 * (u - 3))
                            if prep and hg == 0 and u == 14:
                                remainder(b + 2, 0)
                            if prep and hg == 0 and u == 15:
                                second_half_part(b + 2)
                            if prep and hg == 1 and u in (5, 7):
                                remainder(b + 2, 1 if u == 5 else 2)
                            maxima(n, hg, u, 2, last)
                            if u % 2 == 1:
                                k = (NU * hg + u - 3) // 2
                                if k >= 0:
                                    unit_sum(b, k)
                                elif not first:
                                    unit_sum(b - 1, INNER - 1)

                dve.sem_inc(a_free, 2)
                dve.sem_inc(o_free, 1)
                dve.sem_inc(m_free, 1)
                dve.sem_inc(r_free, 2)
                nc.vector.memset(qst[:].bitcast(F32), 0.0).then_inc(s_qz, 1)
                link(nc.vector.memset(vrow[:], 0.0))
                link(nc.vector.memset(vrow[:, :, :, D:D + 1], 1.0))
                link(nc.vector.memset(ep[:, 0], 0.0))
                dve.wait_ge(c_x[0], 32)
                statistics(0, 2)
                inverse(0, 2, 0)
                dve.wait_ge(c_wT, 1)
                nc.vector.tensor_copy(wT[:].rearrange("p n f -> p (n f)"), ps_b[:, 0, 0:3 * H]).then_inc(c_wTc, 1)
                normal(0, 0)
                normal(0, 2)
                dve.wait_ge(c_cst, 16 * NCST)
                nc.vector.tensor_scalar(colc[:, 0:1], colb[:, 0:1], SCALE, None, ALU.mult).then_inc(c_col, 1)
                nc.vector.tensor_copy(colc[:, 1:2], colb[:, 1:2]).then_inc(c_col, 1)
                nc.vector.tensor_tensor(colc[:, 2:3], colb[:, 1:2], colb[:, 2:3], ALU.add).then_inc(c_col, 1)
                nc.vector.tensor_tensor(colc[:, 3:4], colb[:, 1:2], colb[:, 3:4], ALU.add).then_inc(c_col, 1)
                copy_xT(0, FIRST_BANKS[0][0])
                nc.vector.tensor_copy(wo_t[:], ps_b[:, 0, 3 * H:4 * H]).then_inc(c_wTc, 1)
                band0 = XOFF - LEFT
                dve.wait_ge(c_ebT, 1)
                nc.vector.tensor_copy(ep[:, 0, band0:band0 + NPOS], ps_b[0:D, 1, 0:NPOS]).then_inc(c_ep, 1)
                dve.wait_ge(c_ep, 1)
                e_l, e_r = ep[:, 0, band0:band0 + 1], ep[:, 0, band0 + NPOS - 1:band0 + NPOS]
                link(nc.vector.tensor_scalar(ep[:, 0, 0:band0], ep[:, 0, 0:band0], e_l, None, ALU.add))
                link(nc.vector.tensor_scalar(ep[:, 0, band0 + NPOS:XLEN], ep[:, 0, band0 + NPOS:XLEN], e_r, None, ALU.add))
                link(nc.vector.tensor_scalar(ep[:, K_LEFT], ep[:, 0], e_l, None, ALU.subtract))
                link(nc.vector.tensor_scalar(ep[:, K_RIGHT], ep[:, 0], e_r, None, ALU.subtract))
                nc.vector.tensor_copy(eph[:, :, 0], ep).then_inc(c_ep, 1)
                dve.wait_ge(c_ep, 2)
                nc.vector.tensor_tensor(eph[:, :, 1], ep, eph[:, :, 0], ALU.subtract).then_inc(c_ep, 1)
                second_half_part(0)
                remainder(0, 0)
                remainder(0, 1)
                remainder(0, 2)
                dve.wait_ge(c_row, 16 * NROW)
                v_rows(0, FIRST_BANKS[0][3], False)
                normal(1, 0)
                normal(1, 2)
                mlp_inputs(0, FIRST_BANKS[0][4])
                copy_xT(1, FIRST_BANKS[1][0])
                dve.wait_ge(c_x[1], 16)
                statistics(2, B)
                dve.wait_ge(c_ident, 4)
                dve.wait_ge(d_q[0], 16 * NDQ)
                nc.vector.tensor_tensor(bqa[:, 0], qc[:, 0, :, 0].unsqueeze(2).broadcast_to([P, G, BLK, NBLK]),
                                        mask_h[:].unsqueeze(1).unsqueeze(3).broadcast_to([P, G, BLK, NBLK]), ALU.mult).then_inc(g_first, 1)
                nc.vector.tensor_tensor(rows[:, 3], rows[:, 1], rows[:, 2], ALU.add).then_inc(c_row, 1)
                for g in range(NBLK):
                    maximum(g, g, 0, A_BANKS)
                    if g == 1:
                        mlp_inputs(1, FIRST_BANKS[1][4])
                    if g == 9:
                        second_half_part(1)
                max_rows(0, 0)
                for g in range(A0):
                    maximum(NBLK + g, g, 1)
                    if g == 3:
                        v_rows(1, FIRST_BANKS[1][3], True)
                    if g == 7:
                        dve.wait_ge(v_free, 2)
                        nc.vector.memset(ps_o[:], 0.0).then_inc(s_zero, 1)
                inverse(2, B, 1)
                batches(dve, body)
                unit_sum(B - 1, INNER - 1)
                sums(NPAIR * 2 * B - 1, 1)
                divide(misc(B - 1, NMISC + T3, True), NPAIR * 2 * B - 1, 1, 1)
                copy_oT(misc(B - 1, NMISC + OT, True))
                result(misc(B - 1, NMISC + OUT, True), B - 1)

            @block.scalar
            def _(act):
                def diagonal(s, h):
                    r = slot(s)
                    return nc.scalar.activation(bd[r, h], qx[r], ACT.Copy, scale=mask_f[r, G * s + h:G * s + h + 1])

                def ones(s, half):
                    r = slice(64 * s + 32, 64 * s + 64)
                    act.wait_ge(c_ident, 1)
                    nc.scalar.activation(kst[r, half * Q4:(half + 1) * Q4].rearrange("p h k -> p (h k)"),
                                         ident[r, 0:1].broadcast_to([32, Q4 * KW]),
                                         ACT.Copy, bias=1.0, scale=0.0).then_inc(s_ones[s], 1)

                def q_row(p, ps, stored):
                    act.wait_ge(q_full, p + 1)
                    if stored:
                        act.wait_ge(c_outq, NSQ * p)
                        act.wait_ge(c_out, NST * p)
                    nc.scalar.activation(qkf[:, 0:L], ps, ACT.Identity, bias=colc[:, 0:1], scale=SCALE).then_inc(q_free, 1)

                def k_row(p, ps, kind):
                    act.wait_ge(k_full, p + 1)
                    r0, r1 = {K_LEFT: (0, LW), K_MID: (0, L), K_RIGHT: (RBEG, L)}[kind]
                    o = L + KPOS[kind]
                    m = nc.scalar.activation(qkf[:, o + r0:o + r1], ps[:, r0:r1], ACT.Identity, bias=colc[:, 1 + kind:2 + kind], scale=1.0)
                    if kind == K_RIGHT:
                        m.then_inc(k_free, 1)

                def blocked_q(p):
                    act.wait_ge(q_free, p + 1)
                    blocked = qkf[:, 0:L].rearrange("p (g j) -> p j g", j=BLK)
                    nc.scalar.copy(qd[:], blocked).then_inc(c_hb, 1)
                    nc.scalar.copy(qh[:, :, 0], blocked).then_inc(c_hb, 1)

                def first_part(p, k):
                    act.wait_ge(k_free if k else q_free, p + 1)
                    c = slice(L, L + KW) if k else slice(0, L)
                    nc.scalar.copy(parts[:, 0, c], qkf[:, c]).then_inc(c_hi, 1)

                def second_part(p, i):
                    act.wait_ge(c_rem, NREM * p + i + 1)
                    c = (slice(0, L), slice(L, L + KH), slice(L + KH, L + KW))[i]
                    nc.scalar.copy(parts[:, 1, c], rem[:, c]).then_inc(c_mid, 1)

                def body(b, first, last, prep):
                    for u in range(2 * NU):
                        n = 2 * NU * b + u
                        act.wait_ge(b_full, n + 1)
                        if u % 2 == 0:
                            act.wait_ge(p_free, n + 1)
                        nc.scalar.activation(prob[:, u // 2 % 2, u % 2 * 2 * L:(u % 2 + 1) * 2 * L], ps_b[:, u % 2],
                                             ACT.Exp).then_inc(e_done, 1)
                        if u % 2 == 1:
                            k = u // 2
                            act.wait_ge(s_cp, b + 1)
                            act.wait_ge(r_free, INNER * b + k + 1)
                            nc.scalar.activation(relu[:, k % 2], s_cur[:], ACT.Relu, bias=t["b1c"][:, k:k + 1],
                                                 scale=t["w1c"][:, k:k + 1]).then_inc(r_full, 1)
                        if first and 1 <= u <= NREM:
                            second_part(1, u - 1)
                        s, w = u // NU, u % NU
                        if has(2, s, last) and 4 <= w < 10:
                            for h in ((0, 1), (2,), (3, 4), (5,), (6,), (7,))[w - 4]:
                                if h == 0:
                                    act.wait_ge(d_q[s], 16 * NDQ * (b + 2))
                                m = diagonal(s, h)
                            if w == 9:
                                m.then_inc(g_bd, 1)
                        if prep:
                            p = b + 2
                            if (s, w) == (0, 11):
                                q_row(p, ps_m[:], True)
                            if (s, w) == (0, 12):
                                first_part(p, 0)
                            if (s, w) == (0, 13):
                                blocked_q(p)
                            if (s, w) == (0, 15):
                                second_part(p, 0)
                            if s == 1 and w < 3:
                                k_row(p, ps_m[:], (K_LEFT, K_MID, K_RIGHT)[w])
                            if (s, w) == (1, 3):
                                first_part(p, 1)
                            if (s, w) == (1, 10):
                                second_part(p, 1)
                            if (s, w) == (1, 12):
                                second_part(p, 2)

                act.sem_inc(e_done, 2)
                act.sem_inc(p_free, 3)
                act.sem_inc(r_full, 1)
                act.wait_ge(c_var, 1)
                nc.scalar.activation(std[:, 0:2], var[:, 0:2], ACT.Sqrt).then_inc(c_var, 1)
                act.wait_ge(c_col, 4)
                for p in range(2):
                    q_row(p, FIRST_BANKS[p][1], p > 0)
                    blocked_q(p)
                    for kind in (K_LEFT, K_MID, K_RIGHT):
                        k_row(p, FIRST_BANKS[p][2], kind)
                    first_part(p, 0)
                    first_part(p, 1)
                    if p == 0:
                        for i in range(NREM):
                            second_part(p, i)
                        ones(1, 0)
                    act.wait_ge(c_ident, 3)
                    act.wait_ge(d_q[p], 16 * NDQ)
                    for h in range(G):
                        m = diagonal(p, h)
                    m.then_inc(g_bd, 1)
                    if p == 0:
                        ones(1, 1)
                act.wait_ge(c_var, 3)
                nc.scalar.activation(std[:, 2:B], var[:, 2:B], ACT.Sqrt).then_inc(c_var, 1)
                batches(act, body)


_INS = ["L0_attn_hidden_states", "L0_attn_Wq", "L0_attn_bq", "L0_attn_Wk", "L0_attn_bk", "L0_attn_Wv", "L0_attn_bv",
        "L0_attn_Wo", "L0_attn_bo", "L0_attn_dist_emb", "L0_ffn_Win", "L0_ffn_bin_", "L0_ffn_W1", "L0_ffn_b1",
        "L0_ffn_W2", "L0_ffn_b2", "L0_ffn_Wout", "L0_ffn_bout"]


def kernel(**inputs):
    import numpy as _np
    import concourse.bacc as _bacc
    from concourse import mybir as _mybir
    from concourse.bass_utils import run_bass_kernel_spmd as _run

    nc = _bacc.Bacc("TRN2", target_bir_lowering=False, num_devices=1)
    arrays, args = {}, []
    for name in _INS:
        a = _np.ascontiguousarray(inputs[name])
        arrays[f"in_{name}_dram"] = a
        args.append(nc.dram_tensor(f"in_{name}_dram", a.shape, _mybir.dt.from_np(a.dtype), kind="ExternalInput").ap())
    args.append(nc.dram_tensor("out_0_dram", (B, L, H), _mybir.dt.from_np(_np.dtype("float32")), kind="ExternalOutput").ap())
    build(nc, *args)
    r = _run(nc, [arrays], core_ids=[0])
    return r.results[0]["out_0_dram"]
```
